# Optimizing a Trainium2 kernel written in Bass

```python
import numpy as np
import jax
import jax.numpy as jnp

def _softmax(x, axis=-1):
    return jax.nn.softmax(x, axis=axis)
def _gelu(x):
    return jax.nn.gelu(x, approximate=True)
def _silu(x):
    return jax.nn.silu(x)
def _sigmoid(x):
    return jax.nn.sigmoid(x)
def _layernorm(x, axis=-1, eps=1e-5):
    m = jnp.mean(x, axis=axis, keepdims=True)
    v = jnp.var(x, axis=axis, keepdims=True)
    return (x - m) / jnp.sqrt(v + eps)
def _scatter_add(tgt, idx, src, axis=0):
    return tgt.at[idx].add(src)
def _segment_sum(src, seg, n):
    return jax.ops.segment_sum(src, seg, n)

kernel_name = 'mk_metaformer_d1_conv_nchw256_0f2dba'

def setup_inputs(seed: int = 0):
    np.random.seed(seed)
    _w = jnp.asarray
    def _rec_inputs():
        import jax
        import jax.numpy as jnp
        _gk = jax.random.key(seed)
        x = -0.0009896 + 1 * jax.random.normal(jax.random.fold_in(_gk, 1), (2, 256, 56, 56), jnp.float32)
        return x
    x = _rec_inputs()
    def _L0_conv_setup():
        import jax, jax.numpy as jnp
        import numpy as np
        K = 7
        NH = 8

        def _window_start(L, k):
            i = jnp.arange(L)
            return jnp.clip(i - k // 2, 0, L - k)
        key = jax.random.key(seed)
        ks = jax.random.split(key, 5)
        B, C, H, W = (2, 256, 56, 56)
        return {'x': jax.random.normal(ks[0], (B, C, H, W), dtype=jnp.float32), 'w_qkv': jax.random.normal(ks[1], (3 * C, C), dtype=jnp.float32) * 0.02, 'b_qkv': jnp.zeros((3 * C,), dtype=jnp.float32), 'rpb': jax.random.normal(ks[2], (NH, 2 * K - 1, 2 * K - 1), dtype=jnp.float32) * 0.02, 'w_proj': jax.random.normal(ks[3], (C, C), dtype=jnp.float32) * 0.02, 'b_proj': jnp.zeros((C,), dtype=jnp.float32)}
    _L0_conv_all = _L0_conv_setup()
    _L0_conv_in = {k: v for k, v in _L0_conv_all.items() if k in ('w_qkv', 'b_qkv', 'rpb', 'w_proj', 'b_proj', )}
    del _L0_conv_all

    def _L0_ffn_setup():
        import jax, jax.numpy as jnp
        import numpy as np
        TOP_K = 2
        key = jax.random.key(seed)
        ks = jax.random.split(key, 4)
        B, L, D, H, E = (8, 4096, 256, 1024, 8)
        s = 0.02
        return {'x': jax.random.normal(ks[0], (B, L, D), jnp.float32), 'Wg': jax.random.normal(ks[1], (D, E), jnp.float32) * s, 'bg': jnp.zeros((E,), jnp.float32), 'W1': jax.random.normal(ks[2], (E, D, H), jnp.float32) * s, 'b1': jnp.zeros((E, H), jnp.float32), 'W2': jax.random.normal(ks[3], (E, H, D), jnp.float32) * s, 'b2': jnp.zeros((E, D), jnp.float32)}
    _L0_ffn_all = _L0_ffn_setup()
    _L0_ffn_in = {k: v for k, v in _L0_ffn_all.items() if k in ('Wg', 'bg', 'W1', 'b1', 'W2', 'b2', )}
    del _L0_ffn_all

    return {
        "x": x,
        "L0_conv_w_qkv": _L0_conv_in["w_qkv"],
        "L0_conv_b_qkv": _L0_conv_in["b_qkv"],
        "L0_conv_rpb": _L0_conv_in["rpb"],
        "L0_conv_w_proj": _L0_conv_in["w_proj"],
        "L0_conv_b_proj": _L0_conv_in["b_proj"],
        "L0_ffn_Wg": _L0_ffn_in["Wg"],
        "L0_ffn_bg": _L0_ffn_in["bg"],
        "L0_ffn_W1": _L0_ffn_in["W1"],
        "L0_ffn_b1": _L0_ffn_in["b1"],
        "L0_ffn_W2": _L0_ffn_in["W2"],
        "L0_ffn_b2": _L0_ffn_in["b2"],
    }

def reference(x, L0_conv_w_qkv, L0_conv_b_qkv, L0_conv_rpb, L0_conv_w_proj, L0_conv_b_proj, L0_ffn_Wg, L0_ffn_bg, L0_ffn_W1, L0_ffn_b1, L0_ffn_W2, L0_ffn_b2):
    import jax
    import jax.numpy as jnp
    def _L0_conv_ref(x, w_qkv, b_qkv, rpb, w_proj, b_proj):
        import jax, jax.numpy as jnp
        import numpy as np
        K = 7
        NH = 8

        def _window_start(L, k):
            i = jnp.arange(L)
            return jnp.clip(i - k // 2, 0, L - k)
        B, C, H, W = x.shape
        d = C // NH
        scale = d ** (-0.5)
        xh = jnp.transpose(x, (0, 2, 3, 1))
        qkv = xh @ w_qkv.T + b_qkv
        qkv = qkv.reshape(B, H, W, 3, NH, d).transpose(3, 0, 4, 1, 2, 5)
        q = qkv[0] * scale
        k = qkv[1]
        v = qkv[2]
        sh = _window_start(H, K)
        sw = _window_start(W, K)
        ri = sh[:, None] + jnp.arange(K)[None, :]
        ci = sw[:, None] + jnp.arange(K)[None, :]
        kw = k[:, :, ri[:, :, None, None], ci[None, None, :, :], :]
        vw = v[:, :, ri[:, :, None, None], ci[None, None, :, :], :]
        attn = jnp.einsum('bnhwd,bnhiwjd->bnhwij', q, kw)
        bih = ri - jnp.arange(H)[:, None] + (K - 1)
        biw = ci - jnp.arange(W)[:, None] + (K - 1)
        bias = rpb[:, bih[:, :, None, None], biw[None, None, :, :]]
        bias = bias.transpose(0, 1, 3, 2, 4)
        attn = attn + bias[None]
        a = jax.nn.softmax(attn.reshape(B, NH, H, W, K * K), axis=-1)
        a = a.reshape(B, NH, H, W, K, K)
        out = jnp.einsum('bnhwij,bnhiwjd->bnhwd', a, vw)
        out = out.transpose(0, 2, 3, 1, 4).reshape(B, H, W, C)
        out = out @ w_proj.T + b_proj
        return jnp.transpose(out, (0, 3, 1, 2))

    def _L0_ffn_ref(x, Wg, bg, W1, b1, W2, b2):
        import jax, jax.numpy as jnp
        import numpy as np
        TOP_K = 2
        B, L, D = x.shape
        E = W1.shape[0]
        xf = x.reshape(-1, D)
        gate_logits = xf @ Wg + bg
        top_w, top_i = jax.lax.top_k(gate_logits, TOP_K)
        top_w = jax.nn.softmax(top_w, axis=-1)
        w_dense = jnp.sum(jax.nn.one_hot(top_i, E, dtype=xf.dtype) * top_w[..., None], axis=1)
        out = jnp.zeros_like(xf)
        for e in range(E):
            h = jax.nn.gelu(xf @ W1[e] + b1[e], approximate=False)
            out = out + w_dense[:, e:e + 1] * (h @ W2[e] + b2[e])
        return out.reshape(B, L, D)

    def _gn(v, G=32, eps=1e-5):
        B_, C_, H_, W_ = v.shape
        g = v.reshape(B_, G, C_ // G, H_, W_)
        m = jnp.mean(g, axis=(2, 3, 4), keepdims=True)
        s = jnp.var(g, axis=(2, 3, 4), keepdims=True)
        return ((g - m) / jnp.sqrt(s + eps)).reshape(v.shape)

    def _ln_c(v, eps=1e-6):
        m = jnp.mean(v, axis=1, keepdims=True)
        s = jnp.var(v, axis=1, keepdims=True)
        return (v - m) / jnp.sqrt(s + eps)

    def _ln_t(v, eps=1e-5):
        m = jnp.mean(v, axis=-1, keepdims=True)
        s = jnp.var(v, axis=-1, keepdims=True)
        return (v - m) / jnp.sqrt(s + eps)

    def _to_tokens(v):
        B_, C_, H_, W_ = v.shape
        return v.reshape(B_, C_, H_ * W_).transpose(0, 2, 1)
    def _from_tokens(t, like):
        B_, C_, H_, W_ = like.shape
        return t.transpose(0, 2, 1).reshape(B_, C_, H_, W_)

    x = x + _L0_conv_ref(_ln_c(x), L0_conv_w_qkv, L0_conv_b_qkv, L0_conv_rpb, L0_conv_w_proj, L0_conv_b_proj)
    t = _to_tokens(x)
    t = t + _L0_ffn_ref(_ln_t(t), L0_ffn_Wg, L0_ffn_bg, L0_ffn_W1, L0_ffn_b1, L0_ffn_W2, L0_ffn_b2)
    x = _from_tokens(t, x)
    return x


_drawn_inputs = setup_inputs


def setup_inputs(seed=0):
    import zlib

    import numpy as np

    out = dict(_drawn_inputs(seed))
    spreads = {'L0_conv_b_qkv': (0.0, 0.1),
     'L0_conv_b_proj': (0.0, 0.1),
     'L0_ffn_bg': (0.0, 0.1),
     'L0_ffn_b1': (0.0, 0.307),
     'L0_ffn_b2': (0.0, 0.1)}
    factors = {'L0_conv_w_qkv': 3.096, 'L0_conv_rpb': 28.237}
    for name, (base, spread) in spreads.items():
        noise = np.random.default_rng([zlib.crc32(name.encode()), seed]).standard_normal(out[name].shape)
        drawn = base * np.exp(spread * noise) if base else spread * noise
        out[name] = jnp.asarray(drawn.astype(out[name].dtype))
    for name, factor in factors.items():
        out[name] = (out[name] * factor).astype(out[name].dtype)
    return out
```

```python
import concourse.bass as bass
from concourse import mybir
from contextlib import ExitStack

F32 = mybir.dt.float32
F16 = mybir.dt.float16
BF16 = mybir.dt.bfloat16
I32 = mybir.dt.int32
U32 = mybir.dt.uint32
ALU = mybir.AluOpType
ACT = mybir.ActivationFunctionType
AX = mybir.AxisListType

B, C, H, W = 2, 256, 56, 56
TOKENS = B * H * W
KC = C // 128
NH, HD, WIN = 8, 32, 7
HALF = WIN // 2
QR, QC = 8, 14
QT = QR * QC
KR, KCOL = QR + WIN - 1, QC + WIN - 1
KEYS = KR * KCOL
BANDS = H // QR
COLS = W // QC
BAND = QR * W
GROUPS = TOKENS // BAND
TPG = BAND // QT
TILES = TOKENS // QT
KCHUNK = [(0, 5), (5, 5), (10, 4)]
CK = 5 * KCOL
MODC = 24
NEG = -30000.0
BIAS_R, BIAS_C = KR + HALF * 2, KCOL + HALF * 2
PAD_R, PAD_C = BIAS_R + QR - 1, BIAS_C + QC - 1
RPB = 2 * WIN - 1

E, FH = 8, 1024
HC = FH // 128
ST = 256
CHOICES = 2 * TOKENS
NT = (CHOICES + E * (ST - 1)) // ST
SLOTS = NT * ST
HALVES = SLOTS // 128
BLOCKS = 2 * TILES
WSCALE = 64.0
EW = KC * FH
WCH = 512
MAXT = (TOKENS + ST - 1) // ST


def row_offset(r):
    return 0 if r == 0 else (-2 * HALF if r == BANDS - 1 else -HALF)


def key_col(t):
    return min(max(QC * t - HALF, 0), W - KCOL)


def stage_a(nc, x, wqkv, bqk, bv, ident, qk_hi, qk_lo, v_dram):
    with ExitStack() as c:
        def sb(name, shape, dt):
            return c.enter_context(nc.sbuf_tensor(name, shape, dt))

        def sem(name):
            return c.enter_context(nc.semaphore(name))

        id_a = sb("a_ident", [128, 128], F32)
        w_f = sb("a_w", [128, KC, 3 * C], F32)
        w_hi = sb("a_w_hi", [128, KC, 3 * C], F16)
        w_lo = sb("a_w_lo", [128, KC, 3 * C], F16)
        b_qk = sb("a_b_qk", [128, 4], F32)
        b_v = sb("a_b_v", [QT, C], F32)
        eps = sb("a_eps", [QT, 1], F32)
        xg = sb("a_x", [QT, 2, TPG, C], F32)
        xn = sb("a_xn", [QT, 2, TPG, C], F32)
        st6 = sb("a_st6", [QT, 2, TPG, 6], F32)
        st2 = sb("a_st2", [QT, 2, TPG, 2], F32)
        sd = sb("a_sd", [QT, 2, TPG], F32)
        rs = sb("a_rs", [QT, 2, TPG], F32)
        xt_hi = sb("a_xt_hi", [128, 2, KC, BAND], F16)
        xt_lo = sb("a_xt_lo", [128, 2, KC, BAND], F16)
        qk_f = sb("a_qk_f", [128, 2, 4, BAND], F32)
        o_hi = sb("a_o_hi", [128, 2, 4, BAND], F16)
        o_lo = sb("a_o_lo", [128, 2, 4, BAND], F16)
        v_sb = sb("a_v", [QT, 2, TPG, C], F32)
        ps_t = c.enter_context(nc.psum_tensor("a_ps_t", [128, KC, 512], F32))
        ps_q = c.enter_context(nc.psum_tensor("a_ps_q", [128, 4, 512], F32))
        ps_v = c.enter_context(nc.psum_tensor("a_ps_v", [128, 2, 512], F32))

        consts = sem("a_consts")
        ident_in = sem("a_ident_in")
        w_hi_ok = sem("a_w_hi_ok")
        w_ok = sem("a_w_ok")
        eps_ok = sem("a_eps_ok")
        x_in = [sem(f"a_x_in{i}") for i in range(2)]
        stat = sem("a_stat")
        var_ok = sem("a_var_ok")
        sd_ok = sem("a_sd_ok")
        xn_ok = sem("a_xn_ok")
        t_ok = sem("a_t_ok")
        hi_ok = sem("a_hi_ok")
        xt_ok = sem("a_xt_ok")
        q_ok = sem("a_q_ok")
        qf_ok = sem("a_qf_ok")
        qh_ok = sem("a_qh_ok")
        qk_out = sem("a_qk_out")
        v_ok = sem("a_v_ok")
        v_read = sem("a_v_read")
        v_out = sem("a_v_out")
        stored_hi = [sem(f"a_stored_hi{i}") for i in range(2)]
        stored_lo = [sem(f"a_stored_lo{i}") for i in range(2)]
        stored_v = [sem(f"a_stored_v{i}") for i in range(2)]

        def by_row(buf, s, m):
            return buf[:, s, m, :].rearrange("p (r t w) -> p r t w", r=QR, t=COLS)

        def by_tile(buf, s, m):
            return (buf[:, s, m, :].rearrange("p (t r w) -> p r t w", r=QR, t=COLS) if m < 2 else by_row(buf, s, m))

        with nc.Block() as block:

            @block.sync
            def _(sp):
                sp.dma_start(id_a[:, :], ident).then_inc(ident_in, 16)
                sp.dma_start(w_f[:, :, :], wqkv).then_inc(consts, 16)
                sp.dma_start(b_qk[:, :], bqk).then_inc(consts, 16)
                sp.dma_start(b_v[:, :], bv.to_broadcast([QT, C])).then_inc(consts, 16)

                def load(s, tok):
                    sp.dma_start(xg[:, s], x[bass.ds(tok, BAND), :].rearrange("(t p) c -> p t c", p=QT)
                                 ).then_inc(x_in[s], 16)

                def step(s, tok, last):
                    sp.wait_ge(qk_out, s + 1)
                    sp.dma_start(qk_hi[:, :, bass.ds(tok, BAND)], o_hi[:, s]).then_inc(stored_hi[s], 16)
                    sp.dma_start(qk_lo[:, :, bass.ds(tok, BAND)], o_lo[:, s]).then_inc(stored_lo[s], 16)
                    sp.wait_ge(v_out, s + 1)
                    sp.dma_start(v_dram[bass.ds(tok, BAND), :].rearrange("(t p) c -> p t c", p=QT), v_sb[:, s]
                                 ).then_inc(stored_v[s], 16)
                    if not last:
                        load(s, tok + 2 * BAND)

                load(0, 0)
                load(1, BAND)
                with sp.Fori(0, GROUPS // 2 - 1) as i:
                    for s in range(2):
                        step(s, (2 * i + s) * BAND, False)
                    sp.sem_inc(qk_out, -2)
                    sp.sem_inc(v_out, -2)
                for s in range(2):
                    step(s, (GROUPS - 2 + s) * BAND, True)

            @block.vector
            def _(dve):
                dve.memset(eps[:, :], 1e-6).then_inc(eps_ok, 1)
                for s in range(2):
                    dve.sem_inc(stored_v[s], 16)
                dve.wait_ge(consts, 48)
                dve.tensor_copy(w_hi[:, :, :], w_f[:, :, :]).then_inc(w_hi_ok, 1)
                dve.wait_ge(w_hi_ok, 1)
                dve.tensor_tensor(w_lo[:, :, :], w_f[:, :, :], w_hi[:, :, :], ALU.subtract).then_inc(w_ok, 1)

                def normalise(s):
                    dve.wait_ge(x_in[s], 16)
                    dve.sem_inc(x_in[s], -16)
                    for t in range(TPG):
                        last = dve.bn_stats(st6[:, s, t, :], xg[:, s, t, :])
                    last.then_inc(stat, 1)
                    dve.wait_ge(stat, 1)
                    for t in range(TPG):
                        last = dve.bn_aggr(st2[:, s, t, :], st6[:, s, t, :])
                    last.then_inc(var_ok, 1)
                    dve.wait_ge(sd_ok, 1)
                    dve.sem_inc(sd_ok, -1)
                    dve.reciprocal(rs[:, s, :], sd[:, s, :]).then_inc(stat, 1)
                    dve.wait_ge(stat, 2)
                    dve.sem_inc(stat, -2)
                    for t in range(TPG):
                        last = dve.tensor_scalar(xn[:, s, t, :], xg[:, s, t, :], st2[:, s, t, 0:1], rs[:, s, t:t + 1],
                                                 ALU.subtract, ALU.mult)
                    last.then_inc(xn_ok, 1)

                def low_half(s):
                    dve.wait_ge(hi_ok, 1)
                    dve.sem_inc(hi_ok, -1)
                    dve.tensor_tensor(xt_lo[:, s], ps_t[:, :, 0:BAND], xt_hi[:, s], ALU.subtract).then_inc(xt_ok, 1)

                def step(s, last):
                    if not last:
                        normalise(1 - s)
                    for m in range(4):
                        dve.wait_ge(q_ok, m + 1)
                        dve.tensor_scalar(qk_f[:, s, m, :], ps_q[:, m, 0:BAND], b_qk[:, m:m + 1],
                                          HD ** -0.5 if m < 2 else 1.0, ALU.add, ALU.mult).then_inc(qf_ok, 1)
                    dve.sem_inc(q_ok, -4)
                    if not last:
                        low_half(1 - s)
                    dve.wait_ge(stored_v[s], 16)
                    dve.sem_inc(stored_v[s], -16)
                    for t in range(0, TPG, 2):
                        dve.wait_ge(v_ok, t // 2 + 1)
                        dve.tensor_tensor(v_sb[:, s, t:t + 2, :],
                                          ps_v[0:QT, t // 2, :].rearrange("p (t c) -> p t c", t=2),
                                          b_v[:, :].rearrange("p (a c) -> p a c", a=1).to_broadcast([QT, 2, C]),
                                          ALU.add).then_inc(v_out if t else v_read, 1)
                    dve.sem_inc(v_ok, -2)

                normalise(0)
                low_half(0)
                with dve.Fori(0, GROUPS // 2 - 1):
                    for s in range(2):
                        step(s, False)
                step(0, False)
                step(1, True)
                for s in range(2):
                    dve.wait_ge(stored_v[s], 16)

            @block.scalar
            def _(act):
                for s in range(2):
                    act.sem_inc(stored_hi[s], 16)
                act.wait_ge(eps_ok, 1)

                def roots(s):
                    act.wait_ge(var_ok, 1)
                    act.sem_inc(var_ok, -1)
                    act.activation(sd[:, s, :], st2[:, s, :, 1], ACT.Sqrt, bias=eps[:, :]).then_inc(sd_ok, 1)

                def high_half(s):
                    act.wait_ge(t_ok, 1)
                    act.sem_inc(t_ok, -1)
                    act.copy(xt_hi[:, s], ps_t[:, :, 0:BAND]).then_inc(hi_ok, 1)

                def step(s, last):
                    if not last:
                        roots(1 - s)
                    act.wait_ge(stored_hi[s], 16)
                    act.sem_inc(stored_hi[s], -16)
                    for m in range(4):
                        act.wait_ge(qf_ok, m + 1)
                        act.copy(by_tile(o_hi, s, m), by_row(qk_f, s, m)).then_inc(qh_ok, 1)
                    act.sem_inc(qf_ok, -4)
                    if not last:
                        high_half(1 - s)

                roots(0)
                high_half(0)
                with act.Fori(0, GROUPS // 2 - 1):
                    for s in range(2):
                        step(s, False)
                step(0, False)
                step(1, True)
                for s in range(2):
                    act.wait_ge(stored_hi[s], 16)

            @block.gpsimd
            def _(pool):
                for s in range(2):
                    pool.sem_inc(stored_lo[s], 16)
                with pool.Fori(0, GROUPS // 2):
                    for s in range(2):
                        pool.wait_ge(stored_lo[s], 16)
                        pool.sem_inc(stored_lo[s], -16)
                        for m in range(4):
                            pool.wait_ge(qh_ok, m + 1)
                            last = pool.tensor_tensor(by_tile(o_lo, s, m), by_row(qk_f, s, m), by_tile(o_hi, s, m),
                                                      ALU.subtract)
                        last.then_inc(qk_out, 1)
                        pool.sem_inc(qh_ok, -4)
                for s in range(2):
                    pool.wait_ge(stored_lo[s], 16)

            @block.tensor
            def _(pe):
                pe.wait_ge(ident_in, 16)
                parts = ((w_hi, xt_hi), (w_hi, xt_lo), (w_lo, xt_hi))

                def transposes(s):
                    pe.wait_ge(xn_ok, 1)
                    pe.sem_inc(xn_ok, -1)
                    for k in range(KC):
                        for t in range(TPG):
                            last = pe.transpose(ps_t[:, k, t * QT:(t + 1) * QT], xn[:, s, t, k * 128:(k + 1) * 128],
                                                id_a[0:QT, 0:QT])
                    last.then_inc(t_ok, 1)

                def step(s, last):
                    pe.wait_ge(xt_ok, 1)
                    pe.sem_inc(xt_ok, -1)
                    for m in range(4):
                        for n in range(3 * KC):
                            (w, xx), k = parts[n % 3], n // 3
                            mm = pe.matmul(ps_q[:, m, 0:BAND], w[:, k, m * 128:(m + 1) * 128], xx[:, s, k, :],
                                           start=n == 0, stop=n == 3 * KC - 1)
                        mm.then_inc(q_ok, 1)
                    if not last:
                        transposes(1 - s)
                    for t in range(TPG):
                        if last and t % 2 == 0:
                            pe.wait_ge(v_read, GROUPS - 1 + t // 2)
                        for n in range(3 * KC):
                            (w, xx), k = parts[n % 3], n // 3
                            mm = pe.matmul(ps_v[0:QT, t // 2, (t % 2) * C:(t % 2 + 1) * C],
                                           xx[:, s, k, t * QT:(t + 1) * QT], w[:, k, 2 * C:3 * C],
                                           start=n == 0, stop=n == 3 * KC - 1)
                        if t % 2:
                            mm.then_inc(v_ok, 1)

                transposes(0)
                pe.wait_ge(w_ok, 1)
                with pe.Fori(0, GROUPS // 2 - 1):
                    for s in range(2):
                        step(s, False)
                step(0, False)
                step(1, True)




def stage_b(nc, qk_hi, qk_lo, v_dram, rpb, q_mask, k_mask, ident, w1, w2, rpb_pad, rpb_cols, attn, w1s, w2s):
    with ExitStack() as c:
        def sb(name, shape, dt):
            return c.enter_context(nc.sbuf_tensor(name, shape, dt))

        def sem(name):
            return c.enter_context(nc.semaphore(name))

        id_b = sb("b_ident", [128, 128], F32)
        bias = sb("b_bias", [QT, NH, BIAS_R, BIAS_C], F32)
        q_st = sb("b_q", [128, 2, NH, BAND], F16)
        k_st = sb("b_k", [128, 2, NH, KR * W], F16)
        v_st = sb("b_v", [CK, 4, 3, C], F32)
        s_sb = sb("b_s", [QT, 4, KEYS], F32)
        p_sb = sb("b_p", [QT, 4, KEYS], F32)
        pt_sb = sb("b_pt", [CK, 2, 3, QT], F32)
        neg_max = sb("b_neg_max", [QT, 2, NH], F32)
        total = sb("b_total", [QT, 2, NH], F32)
        inv = sb("b_inv", [QT, 2, NH], F32)
        o_sb = sb("b_o", [QT, 2, C], F32)
        c64 = sb("b_c64", [128, WCH], F32)
        w_in = sb("b_w_in", [128, 2, WCH], F32)
        pad = s_sb[0:NH].rearrange("h a n -> h (a n)")[:, 0:PAD_R * PAD_C].rearrange("h (y x) -> h y x", x=PAD_C)
        ps_s = c.enter_context(nc.psum_tensor("b_ps_s", [128, 4, 512], F32))
        ps_p = c.enter_context(nc.psum_tensor("b_ps_p", [128, 2, 512], F32))
        ps_o = c.enter_context(nc.psum_tensor("b_ps_o", [128, 2, 512], F32))

        ident_in = sem("b_ident_in")
        pad_zero = sem("b_pad_zero")
        pad_in = sem("b_pad_in")
        bias_in = sem("b_bias_in")
        q_mask_in = sem("b_q_mask_in")
        band_in = [sem(f"b_band_in{i}") for i in range(2)]
        v_in = [sem(f"b_v_in{i}") for i in range(4)]
        clear = sem("b_clear")
        s_ok = sem("b_s_ok")
        m_ok = sem("b_m_ok")
        p_ok = sem("b_p_ok")
        t_ok_act = sem("b_t_ok_act")
        t_ok_dve = sem("b_t_ok_dve")
        pt_ok_act = sem("b_pt_ok_act")
        pt_ok_dve = sem("b_pt_ok_dve")
        o_ok = sem("b_o_ok")
        inv_ok = sem("b_inv_ok")
        o_out = sem("b_o_out")
        stored = [sem(f"b_stored{i}") for i in range(2)]
        w_ld = [sem(f"b_w_ld{i}") for i in range(2)]
        w_st = sem("b_w_st")

        grid = attn.rearrange("(b h w) c -> b h w c", b=B, h=H)
        v_grid = v_dram.rearrange("(b h w) c -> b h w c", b=B, h=H)
        TP = 2 * COLS
        NHT = TP * NH

        with nc.Block() as block:

            @block.sync
            def _(sp):
                sp.dma_start(id_b[:, :], ident).then_inc(ident_in, 16)
                for s in range(2):
                    sp.dma_start(q_st[96:128, s], q_mask.rearrange("p (a n) -> p a n", a=1).to_broadcast([32, NH, BAND])
                                 ).then_inc(q_mask_in, 16)

                def load_band(s, r, r0):
                    cls = 0 if isinstance(r, int) and r == 0 else (2 if isinstance(r, int) and r == BANDS - 1 else 1)
                    q0 = s * H * W + r * BAND
                    k0 = s * H * W + r0 * W
                    for part, src in enumerate((qk_hi, qk_hi, qk_lo)):
                        for m in range(2):
                            sp.dma_start(q_st[32 * part:32 * part + 32, s, 4 * m:4 * m + 4, :],
                                         src[:, m, bass.ds(q0, BAND)].rearrange("(h d) n -> d h n", d=HD)
                                         ).then_inc(band_in[s], 16)
                    for part, src in enumerate((qk_hi, qk_lo, qk_hi)):
                        for m in range(2):
                            sp.dma_start(k_st[32 * part:32 * part + 32, s, 4 * m:4 * m + 4, :],
                                         src[:, 2 + m, bass.ds(k0, KR * W)].rearrange("(h d) n -> d h n", d=HD)
                                         ).then_inc(band_in[s], 16)
                    sp.dma_start(k_st[96:128, s], k_mask[cls].rearrange("p (a n) -> p a n", a=1
                                                                      ).to_broadcast([32, NH, KR * W])
                                 ).then_inc(band_in[s], 16)

                def load_v(s, t, r0):
                    for j, (a, n) in enumerate(KCHUNK):
                        sp.dma_start(v_st[0:n * KCOL, t, j, :],
                                     v_grid[s, bass.ds(r0 + a, n), key_col(t):key_col(t) + KCOL, :]
                                     ).then_inc(v_in[t], 16)

                def pair(r, r0, r_next, r0_next):
                    for s in range(2):
                        for t in range(COLS):
                            n = s * COLS + t
                            sp.wait_ge(o_out, n + 1)
                            sp.dma_start(grid[s, bass.ds(r * QR, QR), t * QC:(t + 1) * QC, :], o_sb[:, n % 2, :]
                                         ).then_inc(stored[n % 2], 16)
                            if s == 0:
                                load_v(1, t, r0)
                            elif r_next is not None:
                                load_v(0, t, r0_next)
                        if r_next is not None:
                            load_band(s, r_next, r0_next)
                    sp.sem_inc(o_out, -TP)

                load_band(0, 0, 0)
                for t in range(COLS):
                    load_v(0, t, 0)

                sp.wait_ge(pad_zero, 1)
                sp.dma_start(pad[:, QR - 1:QR - 1 + RPB, QC - 1:QC - 1 + RPB], rpb).then_inc(pad_in, 16)
                sp.wait_ge(pad_in, 16)
                sp.dma_start(rpb_pad, pad).then_inc(pad_in, 16)
                sp.wait_ge(pad_in, 32)
                for j in range(QC):
                    sp.dma_start(rpb_cols[j], rpb_pad[:, :, QC - 1 - j:QC - 1 - j + BIAS_C]).then_inc(pad_in, 16)
                sp.wait_ge(pad_in, 32 + 16 * QC)
                for i in range(QR):
                    sp.dma_start(bias[i * QC:(i + 1) * QC], rpb_cols[:, :, QR - 1 - i:QR - 1 - i + BIAS_R, :]
                                 ).then_inc(bias_in, 16)
                load_band(1, 0, 0)

                pair(0, 0, 1, QR - HALF)
                with sp.Fori(1, BANDS - 2) as r:
                    pair(r, r * QR - HALF, r + 1, (r + 1) * QR - HALF)
                pair(BANDS - 2, (BANDS - 2) * QR - HALF, BANDS - 1, H - KR)
                pair(BANDS - 1, H - KR, None, None)

            @block.tensor
            def _(pe):
                pe.wait_ge(ident_in, 16)
                pe.wait_ge(clear, 1)
                pe.wait_ge(q_mask_in, 32)

                def band_of(j):
                    return j // (COLS * NH)

                def scores(j):
                    s, t, h = band_of(j), j // NH % COLS, j % NH
                    if j % (COLS * NH) == 0:
                        pe.wait_ge(band_in[s], 13 * 16)
                        pe.sem_inc(band_in[s], -13 * 16)
                    q = q_st[:, s, h, t * QT:(t + 1) * QT]
                    k = k_st[:, s, h, :].rearrange("p (r w) -> p r w", w=W)[:, :, key_col(t):key_col(t) + KCOL]
                    pe.matmul(ps_s[0:QT, j % 4, 0:KEYS], q, k, start=True, stop=True).then_inc(s_ok, 1)

                def transposes(j):
                    pe.wait_ge(p_ok, j + 1)
                    for n, (a, rows) in enumerate(KCHUNK):
                        last = pe.transpose(ps_p[0:rows * KCOL, j % 2, n * QT:(n + 1) * QT],
                                            p_sb[:, j % 4, a * KCOL:(a + rows) * KCOL], id_b[0:QT, 0:QT])
                    last.then_inc(t_ok_dve if j % 2 else t_ok_act, 1)

                def values(j):
                    n, h = j // NH, j % NH
                    t = n % COLS
                    pe.wait_ge(pt_ok_dve if j % 2 else pt_ok_act, j // 2 + 1)
                    if h == 0:
                        pe.wait_ge(v_in[t], 48)
                        pe.sem_inc(v_in[t], -48)
                    for m, (a, rows) in enumerate(KCHUNK):
                        last = pe.matmul(ps_o[0:QT, n % 2, h * HD:(h + 1) * HD], pt_sb[0:rows * KCOL, j % 2, m, :],
                                         v_st[0:rows * KCOL, t, m, h * HD:(h + 1) * HD], start=m == 0, stop=m == 2)
                    if h == NH - 1:
                        last.then_inc(o_ok, 1)

                def pair(last):
                    for j in range(NHT):
                        if j + 3 < NHT:
                            scores(j + 3)
                        elif not last:
                            scores(j + 3 - NHT)
                        transposes(j)
                        if j:
                            values(j - 1)
                    values(NHT - 1)
                    pe.sem_inc(p_ok, -NHT)
                    for q in (pt_ok_act, pt_ok_dve):
                        pe.sem_inc(q, -NHT // 2)

                for j in range(3):
                    scores(j)
                with pe.Fori(0, BANDS - 1):
                    pair(False)
                pair(True)

            @block.vector
            def _(dve):
                dve.memset(ps_p[:, :, :], 0.0).then_inc(clear, 1)
                for s in range(2):
                    dve.sem_inc(stored[s], 16)
                dve.wait_ge(bias_in, 16 * QR)

                def bias_and_max(j, off):
                    n, h, t = j // NH, j % NH, j // NH % COLS
                    y, xx = off + WIN - 1, key_col(t) - t * QC + WIN - 1
                    dve.wait_ge(s_ok, j + 1)
                    dve.tensor_tensor_reduce(
                        out=s_sb[:, j % 4, :].rearrange("p (r w) -> p r w", w=KCOL),
                        in0=ps_s[0:QT, j % 4, 0:KEYS].rearrange("p (r w) -> p r w", w=KCOL),
                        in1=bias[:, h, y:y + KR, xx:xx + KCOL], scale=-1.0, scalar=3.0e38, op0=ALU.add, op1=ALU.min,
                        accum_out=neg_max[:, n % 2, h:h + 1]).then_inc(m_ok, 1)

                def evacuate(j):
                    dve.wait_ge(t_ok_dve, j // 2 + 1)
                    dve.tensor_copy(pt_sb[:, 1, :, :], ps_p[0:CK, 1, 0:3 * QT].rearrange("p (c q) -> p c q", c=3)
                                    ).then_inc(pt_ok_dve, 1)

                def normalise(n):
                    dve.wait_ge(o_ok, n + 1)
                    dve.reciprocal(inv[:, n % 2, :], total[:, n % 2, :]).then_inc(inv_ok, 1)
                    dve.wait_ge(stored[n % 2], 16)
                    dve.sem_inc(stored[n % 2], -16)
                    dve.wait_ge(inv_ok, n + 1)
                    dve.tensor_tensor(o_sb[:, n % 2, :].rearrange("p (h d) -> p h d", h=NH),
                                      ps_o[0:QT, n % 2, 0:C].rearrange("p (h d) -> p h d", h=NH),
                                      inv[:, n % 2, :].rearrange("p (h a) -> p h a", a=1).to_broadcast([QT, NH, HD]),
                                      ALU.mult).then_inc(o_out, 1)

                def pair(off):
                    for j in range(NHT + 4):
                        if j < NHT:
                            bias_and_max(j, off)
                        if 2 <= j < NHT + 2 and j % 2:
                            evacuate(j - 2)
                        if j > 3 and j % NH == 3:
                            normalise(j // NH - 1)
                    for q, n in ((s_ok, NHT), (t_ok_dve, NHT // 2), (o_ok, TP), (inv_ok, TP)):
                        dve.sem_inc(q, -n)

                pair(row_offset(0))
                with dve.Fori(1, BANDS - 1):
                    pair(row_offset(1))
                pair(row_offset(BANDS - 1))
                for s in range(2):
                    dve.wait_ge(stored[s], 16)

            @block.scalar
            def _(act):
                def exponential(j):
                    n, h = j // NH, j % NH
                    act.wait_ge(m_ok, j + 1)
                    act.activation(p_sb[:, j % 4, :], s_sb[:, j % 4, :], ACT.Exp, bias=neg_max[:, n % 2, h:h + 1],
                                   scale=-1.0, accum_out=total[:, n % 2, h:h + 1]).then_inc(p_ok, 1)

                def evacuate(j):
                    act.wait_ge(t_ok_act, j // 2 + 1)
                    act.copy(pt_sb[:, 0, :, :], ps_p[0:CK, 0, 0:3 * QT].rearrange("p (c q) -> p c q", c=3)
                             ).then_inc(pt_ok_act, 1)

                with act.Fori(0, BANDS):
                    for j in range(NHT + 2):
                        if j < NHT:
                            exponential(j)
                        if j >= 2 and j % 2 == 0:
                            evacuate(j - 2)
                    act.sem_inc(m_ok, -NHT)
                    act.sem_inc(t_ok_act, -NHT // 2)

            @block.gpsimd
            def _(pool):
                pool.memset(pad, 0.0).then_inc(pad_zero, 1)

                pool.memset(c64[:, :], WSCALE).then_inc(w_st, 1)
                pool.wait_ge(w_st, 1)
                pool.sem_inc(w_st, -1)

                def split(dst, s, e, k, loads):
                    hi, lo = (dst[:, bass.ds(e, 1), n, k * WCH:(k + 1) * WCH].rearrange("p a n -> p (a n)")
                              for n in range(2))
                    pool.wait_ge(w_ld[s], 16 * loads)
                    pool.tensor_tensor(w_in[:, s], w_in[:, s], c64[:, :], ALU.mult).then_inc(w_st, 1)
                    pool.wait_ge(w_st, 1)
                    pool.tensor_copy(hi, w_in[:, s]).then_inc(w_st, 1)
                    pool.wait_ge(w_st, 2)
                    pool.tensor_tensor(lo, w_in[:, s], hi, ALU.subtract).then_inc(w_st, 1)
                    pool.wait_ge(w_st, 3)
                    pool.sem_inc(w_st, -3)

                for mat, (dst, src) in enumerate(((w1s, w1), (w2s, w2))):
                    def load(e, k):
                        pool.dma_start(w_in[:, k % 2], src[:, bass.ds(e, 1), k * WCH:(k + 1) * WCH
                                                           ].rearrange("p a n -> p (a n)")).then_inc(w_ld[k % 2], 16)
                    with pool.Fori(0, E) as e:
                        load(e, 0)
                        for k in range(EW // WCH):
                            if k + 1 < EW // WCH:
                                load(e, k + 1)
                            split(dst, k % 2, e, k, (mat * E + e) * (EW // WCH // 2) + k // 2 + 1)


def stage_c(nc, x, attn, wproj, bproj, wg, bg, ident, x1_dram, xs_dram, logits):
    with ExitStack() as c:
        def sb(name, shape, dt):
            return c.enter_context(nc.sbuf_tensor(name, shape, dt))

        def sem(name):
            return c.enter_context(nc.semaphore(name))

        id_c = sb("c_ident", [128, 128], F32)
        w_p = sb("c_w_p", [128, KC, C], F32)
        w_g = sb("c_w_g", [128, KC, E], F32)
        b_p = sb("c_b_p", [QT, C], F32)
        b_g = sb("c_b_g", [QT, E], F32)
        eps = sb("c_eps", [QT, 1], F32)
        a_sb = sb("c_a", [QT, 2, TPG, C], F32)
        x_sb = sb("c_x", [QT, 2, TPG, C], F32)
        x1 = sb("c_x1", [QT, 2, TPG, C], F32)
        xn = sb("c_xn", [QT, 2, TPG, C], F32)
        xs = sb("c_xs", [QT, 2, TPG, 2, C], F16)
        at = sb("c_at", [128, KC, BAND], F32)
        xt = sb("c_xt", [128, KC, BAND], F32)
        st6 = sb("c_st6", [QT, TPG, 6], F32)
        st2 = sb("c_st2", [QT, 2, TPG, 2], F32)
        sd = sb("c_sd", [QT, 2, TPG], F32)
        rs = sb("c_rs", [QT, 2, TPG], F32)
        ps_a = c.enter_context(nc.psum_tensor("c_ps_a", [128, KC, 512], F32))
        ps_p = c.enter_context(nc.psum_tensor("c_ps_p", [128, 2, 512], F32))
        ps_x = c.enter_context(nc.psum_tensor("c_ps_x", [128, KC, 512], F32))
        ps_g = c.enter_context(nc.psum_tensor("c_ps_g", [128, 2, 512], F32))

        w_in = sem("c_w_in")
        bp_in = sem("c_bp_in")
        bg_in = sem("c_bg_in")
        eps_ok = sem("c_eps_ok")
        a_in = [sem(f"c_a_in{i}") for i in range(2)]
        x_in = [sem(f"c_x_in{i}") for i in range(2)]
        a_tr = sem("c_a_tr")
        a_ev = sem("c_a_ev")
        xb_ok = sem("c_xb_ok")
        p_ok = sem("c_p_ok")
        stat = sem("c_stat")
        var_ok = sem("c_var_ok")
        sd_ok = sem("c_sd_ok")
        xn_ok = sem("c_xn_ok")
        x_tr = sem("c_x_tr")
        x_ev = sem("c_x_ev")
        hi_ok = sem("c_hi_ok")
        out_ok = sem("c_out_ok")
        g_ok = sem("c_g_ok")
        st_x1 = [sem(f"c_st_x1{i}") for i in range(2)]
        st_xs = [sem(f"c_st_xs{i}") for i in range(2)]

        def rows(t, tok):
            return t[bass.ds(tok, BAND), :].rearrange("(t p) c -> p t c", p=QT)

        with nc.Block() as block:

            @block.sync
            def _(sp):
                def load(s, tok):
                    sp.dma_start(a_sb[:, s], rows(attn, tok)).then_inc(a_in[s], 16)
                    sp.dma_start(x_sb[:, s], rows(x, tok)).then_inc(x_in[s], 16)

                def step(s, tok, last):
                    sp.wait_ge(out_ok, s + 1)
                    sp.dma_start(rows(x1_dram, tok), x1[:, s]).then_inc(st_x1[s], 16)
                    sp.dma_start(rows(xs_dram, tok), xs[:, s].rearrange("p t a c -> p t (a c)")).then_inc(st_xs[s], 16)
                    if not last:
                        load(s, tok + 2 * BAND)

                load(0, 0)
                for dst, src in ((w_p[:, :, :], wproj), (w_g[:, :, :], wg), (id_c[:, :], ident)):
                    sp.dma_start(dst, src).then_inc(w_in, 16)
                sp.dma_start(b_p[:, :], bproj.to_broadcast([QT, C])).then_inc(bp_in, 16)
                sp.dma_start(b_g[:, :], bg.to_broadcast([QT, E])).then_inc(bg_in, 16)
                load(1, BAND)
                with sp.Fori(0, GROUPS // 2 - 1) as i:
                    for s in range(2):
                        step(s, (2 * i + s) * BAND, False)
                    sp.sem_inc(out_ok, -2)
                for s in range(2):
                    step(s, (GROUPS - 2 + s) * BAND, True)

            @block.tensor
            def _(pe):
                pe.wait_ge(w_in, 48)

                def transposes(dst, src, done):
                    for k in range(KC):
                        for t in range(TPG):
                            last = pe.transpose(dst[:, k, t * QT:(t + 1) * QT], src[:, t, k * 128:(k + 1) * 128],
                                                id_c[0:QT, 0:QT])
                    last.then_inc(done, 1)

                def turn_attention(s):
                    pe.wait_ge(a_in[s], 16)
                    pe.sem_inc(a_in[s], -16)
                    transposes(ps_a, a_sb[:, s], a_tr)

                def project():
                    pe.wait_ge(a_ev, 1)
                    pe.sem_inc(a_ev, -1)
                    for t in range(TPG):
                        for k in range(KC):
                            last = pe.matmul(ps_p[0:QT, t // 2, (t % 2) * C:(t % 2 + 1) * C],
                                             at[:, k, t * QT:(t + 1) * QT], w_p[:, k, :], start=k == 0, stop=k == KC - 1)
                    last.then_inc(p_ok, 1)

                def turn_xn(s):
                    pe.wait_ge(xn_ok, 1)
                    pe.sem_inc(xn_ok, -1)
                    transposes(ps_x, xn[:, s], x_tr)

                def gate(s):
                    pe.wait_ge(x_ev, 1)
                    pe.sem_inc(x_ev, -1)
                    for t in range(TPG):
                        for k in range(KC):
                            last = pe.matmul(ps_g[0:QT, s, t * E:(t + 1) * E], xt[:, k, t * QT:(t + 1) * QT], w_g[:, k, :],
                                             start=k == 0, stop=k == KC - 1)
                    last.then_inc(g_ok, 1)

                def step(s, last):
                    if not last:
                        turn_attention(1 - s)
                    turn_xn(s)
                    if not last:
                        project()
                    gate(s)

                turn_attention(0)
                project()
                with pe.Fori(0, GROUPS // 2 - 1):
                    for s in range(2):
                        step(s, False)
                step(0, False)
                step(1, True)

            @block.scalar
            def _(act):
                for s in range(2):
                    act.sem_inc(st_xs[s], 16)
                act.wait_ge(eps_ok, 1)

                def take(dst, src, ready, done):
                    act.wait_ge(ready, 1)
                    act.sem_inc(ready, -1)
                    act.copy(dst, src).then_inc(done, 1)

                def roots(s):
                    act.wait_ge(var_ok, 1)
                    act.sem_inc(var_ok, -1)
                    act.activation(sd[:, s, :], st2[:, s, :, 1], ACT.Sqrt, bias=eps[:, :]).then_inc(sd_ok, 1)

                def high_half(s):
                    act.wait_ge(st_xs[s], 16)
                    act.sem_inc(st_xs[s], -16)
                    act.copy(xs[:, s, :, 0, :], xn[:, s]).then_inc(hi_ok, 1)

                def step(s, last):
                    if not last:
                        take(at[:, :, :], ps_a[:, :, 0:BAND], a_tr, a_ev)
                    take(xt[:, :, :], ps_x[:, :, 0:BAND], x_tr, x_ev)
                    high_half(s)
                    if not last:
                        roots(1 - s)

                take(at[:, :, :], ps_a[:, :, 0:BAND], a_tr, a_ev)
                roots(0)
                with act.Fori(0, GROUPS // 2 - 1):
                    for s in range(2):
                        step(s, False)
                step(0, False)
                step(1, True)
                for s in range(2):
                    act.wait_ge(st_xs[s], 16)

            @block.gpsimd
            def _(pool):
                pool.wait_ge(bp_in, 16)

                def add_bias(s):
                    pool.wait_ge(x_in[s], 16)
                    pool.sem_inc(x_in[s], -16)
                    pool.tensor_tensor(x_sb[:, s], x_sb[:, s], b_p[:, :].rearrange("p (a c) -> p a c", a=1
                                                                                 ).to_broadcast([QT, TPG, C]), ALU.add
                                       ).then_inc(xb_ok, 1)

                def low_half(s):
                    pool.wait_ge(hi_ok, 1)
                    pool.sem_inc(hi_ok, -1)
                    pool.tensor_tensor(xs[:, s, :, 1, :], xn[:, s], xs[:, s, :, 0, :], ALU.subtract).then_inc(out_ok, 1)

                add_bias(0)
                with pool.Fori(0, GROUPS // 2 - 1):
                    for s in range(2):
                        add_bias(1 - s)
                        low_half(s)
                add_bias(1)
                low_half(0)
                low_half(1)

            @block.vector
            def _(dve):
                dve.memset(eps[:, :], 1e-5).then_inc(eps_ok, 1)
                for s in range(2):
                    dve.sem_inc(st_x1[s], 16)
                dve.wait_ge(bg_in, 16)

                def residual_and_norm(s):
                    dve.wait_ge(xb_ok, 1)
                    dve.sem_inc(xb_ok, -1)
                    dve.wait_ge(st_x1[s], 16)
                    dve.sem_inc(st_x1[s], -16)
                    dve.wait_ge(p_ok, 1)
                    dve.sem_inc(p_ok, -1)
                    dve.tensor_tensor(x1[:, s].rearrange("p (b t) c -> p b (t c)", b=2), ps_p[0:QT, :, :],
                                      x_sb[:, s].rearrange("p (b t) c -> p b (t c)", b=2), ALU.add).then_inc(stat, 1)
                    dve.wait_ge(stat, 1)
                    for t in range(TPG):
                        last = dve.bn_stats(st6[:, t, :], x1[:, s, t, :])
                    last.then_inc(stat, 1)
                    dve.wait_ge(stat, 2)
                    for t in range(TPG):
                        last = dve.bn_aggr(st2[:, s, t, :], st6[:, t, :])
                    last.then_inc(var_ok, 1)
                    dve.wait_ge(sd_ok, 1)
                    dve.sem_inc(sd_ok, -1)
                    dve.reciprocal(rs[:, s, :], sd[:, s, :]).then_inc(stat, 1)
                    dve.wait_ge(stat, 3)
                    dve.sem_inc(stat, -3)
                    for t in range(TPG):
                        last = dve.tensor_scalar(xn[:, s, t, :], x1[:, s, t, :], st2[:, s, t, 0:1], rs[:, s, t:t + 1],
                                                 ALU.subtract, ALU.mult)
                    last.then_inc(xn_ok, 1)

                def take_logits(s, tile):
                    dve.wait_ge(g_ok, 1)
                    dve.sem_inc(g_ok, -1)
                    dve.tensor_tensor(logits[:, bass.ds(tile, TPG), :],
                                      ps_g[0:QT, s, 0:TPG * E].rearrange("p (t e) -> p t e", t=TPG),
                                      b_g[:, :].rearrange("p (a e) -> p a e", a=1).to_broadcast([QT, TPG, E]), ALU.add)

                residual_and_norm(0)
                with dve.Fori(0, GROUPS // 2 - 1) as i:
                    for s in range(2):
                        residual_and_norm(1 - s)
                        take_logits(s, (2 * i + s) * TPG)
                residual_and_norm(1)
                take_logits(0, (GROUPS - 2) * TPG)
                take_logits(1, (GROUPS - 1) * TPG)
                for s in range(2):
                    dve.wait_ge(st_x1[s], 16)


def stage_d(nc, logits, consts_f, tri, iota_hi, iota_lo, gates, tok_idx, dst_idx, tile_expert):
    with ExitStack() as c:
        def sb(name, shape, dt):
            return c.enter_context(nc.sbuf_tensor(name, shape, dt))

        def sem(name):
            return c.enter_context(nc.semaphore(name))

        cf = sb("d_consts", [128, D_CONSTS], F32)
        tri_sb = sb("d_tri", [QT, 2, QT], BF16)
        i_hi = sb("d_iota_hi", [QT, HALVES], F32)
        i_lo = sb("d_iota_lo", [QT, 128], F32)
        top = sb("d_top", [QT, 2, TILES], F32)
        eq = sb("d_eq", [QT, TILES, E], F32)
        idx = sb("d_idx", [QT, TILES], F32)
        rest = sb("d_rest", [QT, TILES, E], F32)
        hot = sb("d_hot", [QT, BLOCKS, E], F32)
        hot_b = sb("d_hot_b", [QT, BLOCKS, E], BF16)
        diff = sb("d_diff", [QT, TILES], F32)
        ex = sb("d_ex", [QT, TILES], F32)
        total = sb("d_total", [QT, BLOCKS, E], F32)
        upto = sb("d_upto", [QT, BLOCKS, E], F32)
        ones = sb("d_ones", [QT, BLOCKS], F32)
        fill = sb("d_fill", [QT, E, MAXT], F32)
        n_t = sb("d_n_t", [QT, E], F32)
        n_cum = sb("d_n_cum", [QT, E], F32)
        base = sb("d_base", [QT, E], F32)
        past = sb("d_past", [QT, NT, E - 1], F32)
        te = sb("d_te", [QT, NT], F32)
        slot = sb("d_slot", [QT, BLOCKS], F32)
        slot_i = sb("d_slot_i", [QT, BLOCKS], I32)
        part_i = sb("d_part_i", [QT, 2, BLOCKS], I32)
        part = sb("d_part", [QT, 2, BLOCKS], F32)
        a_hot = sb("d_a_hot", [QT, 4, HALVES], F32)
        b_hot = sb("d_b_hot", [QT, 4, 128], F32)
        f = sb("d_f", [128, HALVES], F32)
        g = sb("d_g", [128, 2, HALVES], F32)
        ps = c.enter_context(nc.psum_tensor("d_ps", [128, 4, 512], F32))
        ps_i = c.enter_context(nc.psum_tensor("d_ps_i", [128, 512], F32))

        iota_m8 = cf[0:QT, 0:E]
        full_at = cf[0:QT, E:E + MAXT]
        tile_no = cf[0:QT, E + MAXT:E + MAXT + NT]
        value = cf[0:QT, E + MAXT + NT:E + MAXT + NT + BLOCKS]
        spare = cf[:, E + MAXT + NT + BLOCKS:E + MAXT + NT + BLOCKS + HALVES]

        c_in = sem("d_c_in")
        tri_in = sem("d_tri_in")
        did = sem("d_did")
        diff_ok = sem("d_diff_ok")
        ex_ok = sem("d_ex_ok")
        hot_ok = sem("d_hot_ok")
        cnt_ok = sem("d_cnt_ok")
        pair_ok = sem("d_pair_ok")
        pair_used = sem("d_pair_used")

        def per_e(t2):
            return t2.rearrange("p (a e) -> p a e", a=1)

        def over_e(t2, n):
            return t2.rearrange("p (t a) -> p t a", a=1).to_broadcast([QT, n, E])

        with nc.Block() as block:

            @block.sync
            def _(sp):
                sp.dma_start(cf[:, :], consts_f).then_inc(c_in, 16)
                sp.dma_start(i_hi[:, :], iota_hi).then_inc(c_in, 16)
                sp.dma_start(i_lo[:, :], iota_lo).then_inc(c_in, 16)
                sp.dma_start(tri_sb[:, :, :], tri).then_inc(tri_in, 16)

            @block.vector
            def _(dve):
                count = [0]

                def link(ins):
                    ins.then_inc(did, 1)
                    count[0] += 1
                    dve.wait_ge(did, count[0])

                dve.wait_ge(c_in, 48)
                link(dve.memset(ones[:, :], 1.0))
                lg = logits[:, :, :]
                for k in range(2):
                    one_hot = hot[:, k * TILES:(k + 1) * TILES, :]
                    link(dve.tensor_reduce(top[:, k, :], lg, AX.X, ALU.max))
                    link(dve.tensor_tensor(eq[:, :, :], lg, over_e(top[:, k, :], TILES), ALU.is_equal))
                    link(dve.tensor_tensor(eq[:, :, :], eq[:, :, :], per_e(iota_m8).to_broadcast([QT, TILES, E]),
                                           ALU.mult))
                    link(dve.tensor_reduce(idx[:, :], eq[:, :, :], AX.X, ALU.min))
                    link(dve.tensor_tensor(one_hot, per_e(iota_m8).to_broadcast([QT, TILES, E]),
                                           over_e(idx[:, :], TILES), ALU.is_equal))
                    if k == 0:
                        link(dve.scalar_tensor_tensor(rest[:, :, :], one_hot, -1e30, lg, ALU.mult, ALU.add))
                        lg = rest[:, :, :]
                dve.tensor_copy(hot_b[:, :, :], hot[:, :, :]).then_inc(hot_ok, 1)
                dve.tensor_tensor(diff[:, :], top[:, 1, :], top[:, 0, :], ALU.subtract).then_inc(diff_ok, 1)
                dve.wait_ge(cnt_ok, 1)
                for k in range(2):
                    link(dve.tensor_copy(total[:, k * TILES:(k + 1) * TILES, :],
                                         ps[0:QT, 2 + k, 0:TILES * E].rearrange("p (t e) -> p t e", e=E)))
                for e in range(E):
                    link(dve.tensor_tensor_scan(upto[:, :, e], ones[:, :], total[:, :, e], 0.0, ALU.mult, ALU.add))
                link(dve.tensor_tensor(fill[:, :, :], upto[:, BLOCKS - 1, :].rearrange("p (e a) -> p e a", a=1
                                                                                   ).to_broadcast([QT, E, MAXT]),
                                       full_at.rearrange("p (a n) -> p a n", a=1).to_broadcast([QT, E, MAXT]),
                                       ALU.is_gt))
                link(dve.tensor_reduce(n_t[:, :], fill[:, :, :], AX.X, ALU.add))
                link(dve.tensor_tensor_scan(n_cum[:, :], ones[:, 0:E], n_t[:, :], 0.0, ALU.mult, ALU.add))
                link(dve.tensor_tensor(base[:, :], n_cum[:, :], n_t[:, :], ALU.subtract))
                link(dve.tensor_scalar(base[:, :], base[:, :], float(ST), None, ALU.mult))
                link(dve.tensor_tensor(past[:, :, :], tile_no.rearrange("p (t a) -> p t a", a=1
                                                                      ).to_broadcast([QT, NT, E - 1]),
                                       per_e(n_cum[:, 0:E - 1]).to_broadcast([QT, NT, E - 1]), ALU.is_ge))
                link(dve.tensor_reduce(te[:, :], past[:, :, :], AX.X, ALU.add))
                link(dve.tensor_copy(tile_expert[0:1, :], te[0:1, :]))
                link(dve.tensor_tensor(upto[:, :, :], upto[:, :, :], total[:, :, :], ALU.subtract))
                for k in range(2):
                    half = upto[:, k * TILES:(k + 1) * TILES, :]
                    link(dve.tensor_tensor(half, ps[0:QT, k, 0:TILES * E].rearrange("p (t e) -> p t e", e=E), half,
                                           ALU.add))
                link(dve.tensor_tensor(upto[:, :, :], upto[:, :, :], per_e(base[:, :]).to_broadcast([QT, BLOCKS, E]),
                                       ALU.add))
                link(dve.tensor_tensor(upto[:, :, :], upto[:, :, :], hot[:, :, :], ALU.mult))
                link(dve.tensor_reduce(slot[:, :], upto[:, :, :], AX.X, ALU.add))
                link(dve.tensor_copy(slot_i[:, :], slot[:, :]))
                link(dve.tensor_scalar(part_i[:, 0, :], slot_i[:, :], 7, None, ALU.arith_shift_right))
                link(dve.tensor_scalar(part_i[:, 1, :], slot_i[:, :], 127, None, ALU.bitwise_and))
                link(dve.tensor_copy(part[:, :, :], part_i[:, :, :]))

                dve.wait_ge(ex_ok, 1)
                link(dve.tensor_scalar(top[:, 0, :], ex[:, :], 1.0, None, ALU.add))
                link(dve.reciprocal(gates[:, 0, :], top[:, 0, :]))
                link(dve.tensor_tensor(gates[:, 1, :], gates[:, 0, :], ex[:, :], ALU.mult))

                def one_hots(j, b):
                    dve.wait_ge(pair_used, j + 1)
                    dve.tensor_scalar(a_hot[:, j, :], i_hi[:, :], part[:, 0, bass.ds(b, 1)], value[:, bass.ds(b, 1)],
                                      ALU.is_equal, ALU.mult)
                    dve.tensor_scalar(b_hot[:, j, :], i_lo[:, :], part[:, 1, bass.ds(b, 1)], None, ALU.is_equal
                                      ).then_inc(pair_ok, 1)

                dve.sem_inc(pair_used, 4)
                with dve.Fori(0, BLOCKS // 4) as i:
                    for j in range(4):
                        one_hots(j, 4 * i + j)
                    dve.sem_inc(pair_used, -4)
                dve.wait_ge(pair_used, 4)
                link(dve.tensor_copy(f[:, :], ps_i[:, 0:HALVES]))
                link(dve.tensor_scalar(g[:, 0, :], f[:, :], 0.0, None, ALU.is_equal))
                link(dve.tensor_tensor(g[:, 0, :], g[:, 0, :], spare, ALU.mult))
                link(dve.tensor_tensor(g[:, 0, :], g[:, 0, :], f[:, :], ALU.add))
                link(dve.tensor_scalar(dst_idx[:, :], g[:, 0, :], -1.0, None, ALU.add))
                link(dve.tensor_scalar(g[:, 1, :], f[:, :], float(TOKENS), -float(TOKENS), ALU.is_gt, ALU.mult))
                link(dve.tensor_tensor(g[:, 1, :], g[:, 1, :], f[:, :], ALU.add))
                link(dve.tensor_scalar(tok_idx[:, :], g[:, 1, :], -1.0, 0.0, ALU.add, ALU.max))

            @block.scalar
            def _(act):
                act.wait_ge(diff_ok, 1)
                act.activation(ex[:, :], diff[:, :], ACT.Exp).then_inc(ex_ok, 1)

            @block.tensor
            def _(pe):
                pe.wait_ge(tri_in, 16)
                pe.wait_ge(hot_ok, 1)
                for n in range(2):
                    for k in range(2):
                        last = pe.matmul(ps[0:QT, 2 * n + k, 0:TILES * E], tri_sb[:, n, :],
                                         hot_b[:, k * TILES:(k + 1) * TILES, :].rearrange("p t e -> p (t e)"),
                                         start=True, stop=True)
                last.then_inc(cnt_ok, 1)

                def block_product(j, first, final):
                    pe.wait_ge(pair_ok, j + 1)
                    pe.matmul(ps_i[:, 0:HALVES], b_hot[:, j, :], a_hot[:, j, :], start=first, stop=final
                              ).then_inc(pair_used, 1)

                for j in range(4):
                    block_product(j, j == 0, False)
                pe.sem_inc(pair_ok, -4)
                with pe.Fori(1, BLOCKS // 4 - 1):
                    for j in range(4):
                        block_product(j, False, False)
                    pe.sem_inc(pair_ok, -4)
                for j in range(4):
                    block_product(j, False, j == 3)


def routing_constants():
    import numpy as np
    p = np.arange(128)[:, None]
    parts = [np.arange(E)[None] - E + 0 * p, ST * np.arange(MAXT)[None] + 0 * p, np.arange(NT)[None] + 0 * p,
             np.arange(BLOCKS)[None] * QT + p + 1, CHOICES + 1 + 128 * np.arange(HALVES)[None] + p]
    tri = np.zeros((QT, 2, QT), np.float32)
    tri[:, 0, :] = np.arange(QT)[:, None] < np.arange(QT)[None]
    tri[:, 1, :] = 1
    return np.concatenate(parts, 1).astype(np.float32), tri


D_CONSTS = E + MAXT + NT + BLOCKS + HALVES


def stage_e(nc, xs_dram, y_dram, w1s, w2s, b1, b2, ident16, tok_idx, dst_idx, tile_expert):
    with ExitStack() as c:
        def sb(name, shape, dt):
            return c.enter_context(nc.sbuf_tensor(name, shape, dt))

        def sem(name):
            return c.enter_context(nc.semaphore(name))

        U = 4
        id_e = sb("e_ident", [128, 128], F16)
        b1_sb = sb("e_b1", [128, E * HC], F32)
        b2_sb = sb("e_b2", [128, E, C], F32)
        xg = sb("e_xg", [128, U, 2, 2 * C], F16)
        xt = sb("e_xt", [128, 2, 2, 4, 128], F16)
        gf = sb("e_gf", [128, 4, ST], F32)
        g_hi = sb("e_g_hi", [128, 2, HC, ST], F16)
        g_lo = sb("e_g_lo", [128, 2, HC, ST], F16)
        y_sb = sb("e_y", [128, 2, 2, C], F32)
        gi = sb("e_gi", [128, U, 2], I32)
        si = sb("e_si", [128, 2, 2], I32)
        ps_x = c.enter_context(nc.psum_tensor("e_ps_x", [128, 2 * 4 * 128], F16))
        ps_h = c.enter_context(nc.psum_tensor("e_ps_h", [128, 4, 512], F32))
        ps_y = c.enter_context(nc.psum_tensor("e_ps_y", [128, 2, 512], F32))

        id_in = sem("e_id_in")
        b1_in = sem("e_b1_in")
        b2_in = sem("e_b2_in")
        idx_ok = sem("e_idx_ok")
        xg_in = [sem(f"e_xg_in{i}") for i in range(U)]
        x_tr = sem("e_x_tr")
        xt_ok = sem("e_xt_ok")
        h_ok = sem("e_h_ok")
        g_ok = sem("e_g_ok")
        hi_ok = sem("e_hi_ok")
        gs_ok = sem("e_gs_ok")
        y_ok = sem("e_y_ok")
        y_out = sem("e_y_out")
        y_done = [sem(f"e_y_done{i}") for i in range(2)]

        with nc.Block() as block:

            @block.sync
            def _(sp):
                sp.dma_start(id_e[:, :], ident16).then_inc(id_in, 16)
                sp.dma_start(b1_sb[:, :], b1).then_inc(b1_in, 16)
                sp.dma_start(b2_sb[:, :, :].rearrange("p e c -> p (e c)"), b2.to_broadcast([128, E * C])
                             ).then_inc(b2_in, 16)

            @block.gpsimd
            def _(pool):
                def fetch_indices(dst, src, n):
                    pool.tensor_copy(dst, src[:, bass.ds(2 * n, 2)]).then_inc(idx_ok, 1)
                    pool.wait_ge(idx_ok, 1)
                    pool.sem_inc(idx_ok, -1)

                def gather(j, n):
                    fetch_indices(gi[:, j, :], tok_idx, n)
                    for h in range(2):
                        pool.indirect_dma_start(out=xg[:, j, h, :], out_offset=None, in_=xs_dram,
                                                in_offset=bass.IndirectOffsetOnAxis(ap=gi[:, j, h:h + 1], axis=0)
                                                ).then_inc(xg_in[j], 16)

                def step(j, n, last):
                    s = j % 2
                    pool.wait_ge(y_out, j + 1)
                    fetch_indices(si[:, s, :], dst_idx, n)
                    for h in range(2):
                        pool.indirect_dma_start(out=y_dram,
                                                out_offset=bass.IndirectOffsetOnAxis(ap=si[:, s, h:h + 1], axis=0),
                                                in_=y_sb[:, s, h, :], in_offset=None).then_inc(y_done[s], 16)
                    if not last:
                        gather(j, n + U)

                for j in range(U):
                    gather(j, j)
                with pool.Fori(0, NT // U - 1) as i:
                    for j in range(U):
                        step(j, U * i + j, False)
                    pool.sem_inc(y_out, -U)
                for j in range(U):
                    step(j, NT - U + j, True)

            @block.tensor
            def _(pe):
                pe.wait_ge(id_in, 16)

                def turn(m, round_):
                    pe.wait_ge(xg_in[m % U], 32 * round_)
                    for h in range(2):
                        for q in range(4):
                            last = pe.transpose(ps_x[:, (4 * h + q) * 128:(4 * h + q + 1) * 128],
                                                xg[:, m % U, h, q * 128:(q + 1) * 128], id_e[:, :])
                    last.then_inc(x_tr, 1)

                def up(m, e, first):
                    s = m % 2
                    pe.wait_ge(xt_ok, 1)
                    pe.sem_inc(xt_ok, -1)
                    for hc in range(HC):
                        if not first or hc >= 4:
                            pe.wait_ge(gs_ok, hc - 3 + (0 if first else HC))
                        n = 0
                        for k in range(KC):
                            for w, p in ((0, 0), (0, 1), (1, 0)):
                                a = k * FH + hc * 128
                                mm = pe.matmul(ps_h[:, hc % 4, 0:ST],
                                               w1s[:, bass.ds(e, 1), w, a:a + 128].rearrange("p a n -> p (a n)"),
                                               xt[:, s, :, 2 * p + k, :], start=n == 0, stop=n == 3 * KC - 1)
                                n += 1
                        mm.then_inc(h_ok, 1)
                    if not first:
                        pe.sem_inc(gs_ok, -HC)

                def down(m, e):
                    s = m % 2
                    for h in range(2):
                        n = 0
                        for hc in range(HC):
                            for g, w in ((g_hi, 0), (g_hi, 1), (g_lo, 0)):
                                a = hc * C
                                mm = pe.matmul(ps_y[:, s, h * C:(h + 1) * C], g[:, s, hc, h * 128:(h + 1) * 128],
                                               w2s[:, bass.ds(e, 1), w, a:a + C].rearrange("p a n -> p (a n)"),
                                               start=n == 0, stop=n == 3 * HC - 1)
                                n += 1
                    mm.then_inc(y_ok, 1)

                def expert(n):
                    return pe.value_load(tile_expert[0:1, bass.ds(n, 1)], min_val=0, max_val=E - 1)

                turn(0, 1)
                up(0, expert(0), True)
                turn(1, 1)
                with pe.Fori(0, NT // U - 1) as i:
                    for j in range(U):
                        up(j + 1, expert(U * i + j + 1), False)
                        turn(j + 2, i + 1 + (j + 2) // U)
                        down(j, expert(U * i + j))
                for j in range(U):
                    n = NT - U + j
                    if j + 1 < U:
                        up(j + 1, expert(n + 1), False)
                    else:
                        pe.wait_ge(gs_ok, HC)
                    if j + 2 < U:
                        turn(j + 2, NT // U)
                    down(j, expert(n))

            @block.scalar
            def _(act):
                act.wait_ge(b1_in, 16)
                with act.Fori(0, NT // 2) as i:
                    for j in range(2):
                        e = act.value_load(tile_expert[0:1, bass.ds(2 * i + j, 1)], min_val=0, max_val=E - 1)
                        for hc in range(HC):
                            act.wait_ge(h_ok, j * HC + hc + 1)
                            act.activation(gf[:, hc % 4, :], ps_h[:, hc % 4, 0:ST], ACT.Gelu,
                                           bias=b1_sb[:, bass.ds(e * HC + hc, 1)], scale=1.0 / WSCALE).then_inc(g_ok, 1)
                    act.sem_inc(h_ok, -2 * HC)

            @block.vector
            def _(dve):
                dve.wait_ge(b2_in, 16)

                def take_x(s):
                    dve.wait_ge(x_tr, 1)
                    dve.sem_inc(x_tr, -1)
                    dve.tensor_copy(xt[:, s].rearrange("p h q n -> p (h q n)").bitcast(F32), ps_x[:, :].bitcast(F32)
                                    ).then_inc(xt_ok, 1)

                def split(s):
                    for hc in range(HC):
                        dve.wait_ge(g_ok, hc + 1)
                        dve.tensor_copy(g_hi[:, s, hc, :], gf[:, hc % 4, :]).then_inc(hi_ok, 1)
                        dve.wait_ge(hi_ok, hc + 1)
                        dve.tensor_tensor(g_lo[:, s, hc, :], gf[:, hc % 4, :], g_hi[:, s, hc, :], ALU.subtract
                                          ).then_inc(gs_ok, 1)
                    dve.sem_inc(g_ok, -HC)
                    dve.sem_inc(hi_ok, -HC)

                def take_y(s, n, scatters):
                    e = dve.value_load(tile_expert[0:1, bass.ds(n, 1)], min_val=0, max_val=E - 1)
                    if scatters is not None:
                        dve.wait_ge(y_done[s], 32 * scatters)
                    dve.wait_ge(y_ok, 1)
                    dve.sem_inc(y_ok, -1)
                    dve.scalar_tensor_tensor(y_sb[:, s], ps_y[:, s, :].rearrange("p (h c) -> p h c", h=2),
                                             1.0 / WSCALE, b2_sb[:, bass.ds(e, 1), :].to_broadcast([128, 2, C]),
                                             ALU.mult, ALU.add).then_inc(y_out, 1)

                take_x(0)
                split(0)
                take_x(1)
                for j in range(2):
                    split(1 - j)
                    take_x(j)
                    take_y(j, j, None)
                with dve.Fori(1, NT // 2 - 1) as i:
                    for j in range(2):
                        split(1 - j)
                        take_x(j)
                        take_y(j, 2 * i + j, i)
                split(1)
                take_y(0, NT - 2, NT // 2 - 1)
                take_y(1, NT - 1, NT // 2 - 1)
                for s in range(2):
                    dve.wait_ge(y_done[s], 32 * (NT // 2))


def stage_f(nc, x1_dram, y_dram, gates, out):
    with ExitStack() as c:
        def sb(name, shape, dt):
            return c.enter_context(nc.sbuf_tensor(name, shape, dt))

        def sem(name):
            return c.enter_context(nc.semaphore(name))

        U = 2
        x1 = sb("f_x1", [QT, U, TPG, C], F32)
        y = sb("f_y", [QT, U, 2, TPG, C], F32)
        t1 = sb("f_t", [QT, U, TPG, C], F32)
        o = sb("f_o", [QT, U, TPG, C], F32)
        in_ok = [sem(f"f_in{i}") for i in range(U)]
        half_ok = sem("f_half")

        stored = [sem(f"f_stored{i}") for i in range(U)]
        used = sem("f_used")

        def rows(t, tok):
            return t[bass.ds(tok, BAND), :].rearrange("(t p) c -> p t c", p=QT)

        with nc.Block() as block:

            @block.sync
            def _(sp):
                def load(s, tok):
                    sp.dma_start(x1[:, s], rows(x1_dram, tok)).then_inc(in_ok[s], 16)
                    for k in range(2):
                        sp.dma_start(y[:, s, k], rows(y_dram, tok + k * TOKENS)).then_inc(in_ok[s], 16)

                for s in range(U):
                    load(s, s * BAND)
                with sp.Fori(0, GROUPS // U - 1) as i:
                    for s in range(U):
                        sp.wait_ge(used, s + 1)
                        sp.dma_start(rows(out, (U * i + s) * BAND), o[:, s]).then_inc(stored[s], 16)
                        load(s, (U * i + s + U) * BAND)
                    sp.sem_inc(used, -U)
                for s in range(U):
                    sp.wait_ge(used, s + 1)
                    sp.dma_start(rows(out, (GROUPS - U + s) * BAND), o[:, s]).then_inc(stored[s], 16)

            @block.vector
            def _(dve):
                for s in range(U):
                    dve.sem_inc(stored[s], 16)
                with dve.Fori(0, GROUPS // U) as i:
                    for s in range(U):
                        dve.wait_ge(in_ok[s], 48)
                        dve.sem_inc(in_ok[s], -48)
                        dve.wait_ge(stored[s], 16)
                        dve.sem_inc(stored[s], -16)
                        for k, (dst, src, done) in enumerate(((t1, x1, half_ok), (o, t1, used))):
                            for t in range(TPG):
                                last = dve.scalar_tensor_tensor(dst[:, s, t, :], y[:, s, k, t, :],
                                                                gates[:, k, bass.ds((U * i + s) * TPG + t, 1)],
                                                                src[:, s, t, :], ALU.mult, ALU.add)
                            last.then_inc(done, 1)
                            if k == 0:
                                dve.wait_ge(half_ok, 1)
                                dve.sem_inc(half_ok, -1)
                for s in range(U):
                    dve.wait_ge(stored[s], 16)


def col_windows(q):
    s = min(max(q - HALF, 0), W - WIN)
    return s, s + WIN


def masks():
    import numpy as np
    q = np.zeros((32, QR, W), np.float16)
    for i in range(QR):
        q[i, i, :] = 1
    for w in range(W):
        q[QR + w % MODC, :, w] = 1
    k = np.full((3, 32, KR, W), NEG, np.float16)
    for cls, r in enumerate((0, 1, BANDS - 1)):
        r0 = QR * r + row_offset(r)
        for i in range(QR):
            s = min(max(QR * r + i - HALF, 0), H - WIN) - r0
            k[cls, i, s:s + WIN, :] = 0
    for w in range(W):
        a, b = col_windows(w)
        k[:, QR + w % MODC, :, a:b] = 0
    return q.reshape(32, QR, COLS, QC).transpose(0, 2, 1, 3).reshape(32, BAND), k.reshape(3, 32, KR * W)


def program(nc, t, out):
    def scratch(name, shape, dt):
        return nc.dram_tensor(name, shape, dt, kind="Internal").ap()

    qk_hi = scratch("qk_hi", [128, 4, TOKENS], F16)
    qk_lo = scratch("qk_lo", [128, 4, TOKENS], F16)
    v_dram = scratch("v_rows", [TOKENS, C], F32)
    rpb_pad = scratch("rpb_pad", [NH, PAD_R, PAD_C], F32)
    rpb_cols = scratch("rpb_cols", [QC, NH, PAD_R, BIAS_C], F32)
    attn = scratch("attn", [TOKENS, C], F32)
    x1 = scratch("x1", [TOKENS, C], F32)
    xs = scratch("xs", [TOKENS, 2 * C], F16)
    y = scratch("y", [CHOICES + SLOTS, C], F32)

    stage_a(nc, t["x"], t["wqkv"], t["bqk"], t["bv"], t["ident"], qk_hi, qk_lo, v_dram)
    with ExitStack() as c:
        w1s = c.enter_context(nc.sbuf_tensor("w1s", [128, E, 2, EW], F16))
        w2s = c.enter_context(nc.sbuf_tensor("w2s", [128, E, 2, EW], F16))
        stage_b(nc, qk_hi, qk_lo, v_dram, t["rpb"], t["q_mask"], t["k_mask"], t["ident"], t["w1"], t["w2"],
                rpb_pad, rpb_cols, attn, w1s, w2s)
        logits = c.enter_context(nc.sbuf_tensor("logits", [QT, TILES, E], F32))
        gates = c.enter_context(nc.sbuf_tensor("gates", [QT, 2, TILES], F32))
        tok_idx = c.enter_context(nc.sbuf_tensor("tok_idx", [128, HALVES], I32))
        dst_idx = c.enter_context(nc.sbuf_tensor("dst_idx", [128, HALVES], I32))
        tile_expert = c.enter_context(nc.sbuf_tensor("tile_expert", [1, NT], I32))
        stage_c(nc, t["x"], attn, t["wproj"], t["bproj"], t["wg"], t["bg"], t["ident"], x1, xs, logits)
        stage_d(nc, logits, t["consts"], t["tri"], t["iota_hi"], t["iota_lo"], gates, tok_idx, dst_idx, tile_expert)
        stage_e(nc, xs, y, w1s, w2s, t["b1"], t["b2"], t["ident16"], tok_idx, dst_idx, tile_expert)
        stage_f(nc, x1, y, gates, out)


def kernel(**inputs):
    import ml_dtypes
    import numpy as np
    import concourse.bacc as bacc
    from concourse.bass_utils import run_bass_kernel_spmd as run

    q_mask, k_mask = masks()
    consts, tri = routing_constants()
    arrays = {
        "x": np.transpose(inputs["x"], (0, 2, 3, 1)).reshape(TOKENS, C),
        "wqkv": inputs["L0_conv_w_qkv"].T.reshape(KC, 128, 3 * C).transpose(1, 0, 2),
        "bqk": inputs["L0_conv_b_qkv"][:2 * C].reshape(4, 128).T,
        "bv": inputs["L0_conv_b_qkv"][2 * C:].reshape(1, C),
        "rpb": inputs["L0_conv_rpb"],
        "wproj": inputs["L0_conv_w_proj"].T.reshape(KC, 128, C).transpose(1, 0, 2),
        "bproj": inputs["L0_conv_b_proj"].reshape(1, C),
        "wg": inputs["L0_ffn_Wg"].reshape(KC, 128, E).transpose(1, 0, 2),
        "bg": inputs["L0_ffn_bg"].reshape(1, E),
        "w1": inputs["L0_ffn_W1"].reshape(E, KC, 128, FH).transpose(2, 0, 1, 3).reshape(128, E, EW),
        "b1": inputs["L0_ffn_b1"].reshape(E * HC, 128).T,
        "w2": inputs["L0_ffn_W2"].reshape(E, HC, 128, C).transpose(2, 0, 1, 3).reshape(128, E, EW),
        "b2": inputs["L0_ffn_b2"].reshape(1, E * C),
        "ident": np.eye(128, dtype=np.float32),
        "ident16": np.eye(128, dtype=np.float16),
        "q_mask": q_mask,
        "k_mask": k_mask,
        "consts": consts,
        "tri": tri.astype(ml_dtypes.bfloat16),
        "iota_hi": np.tile(np.arange(HALVES, dtype=np.float32), (QT, 1)),
        "iota_lo": np.tile(np.arange(128, dtype=np.float32), (QT, 1)),
    }
    arrays = {f"in_{n}": np.ascontiguousarray(a) for n, a in arrays.items()}
    nc = bacc.Bacc("TRN2", target_bir_lowering=False, num_devices=1, dynamic_dma_scratch_size=4096)
    t = {n[3:]: nc.dram_tensor(n, a.shape, mybir.dt.from_np(a.dtype), kind="ExternalInput").ap()
         for n, a in arrays.items()}
    out = nc.dram_tensor("out", [TOKENS, C], F32, kind="ExternalOutput").ap()
    program(nc, t, out)
    got = run(nc, [arrays], core_ids=[0]).results[0]["out"]
    return np.ascontiguousarray(np.transpose(got.reshape(B, H, W, C), (0, 3, 1, 2)))
```

```python
import concourse.bass as bass
from concourse import mybir
from contextlib import ExitStack

F32 = mybir.dt.float32
F16 = mybir.dt.float16
BF16 = mybir.dt.bfloat16
I32 = mybir.dt.int32
U32 = mybir.dt.uint32
ALU = mybir.AluOpType
ACT = mybir.ActivationFunctionType
AX = mybir.AxisListType

B, C, H, W = 2, 256, 56, 56
TOKENS = B * H * W
KC = C // 128
NH, HD, WIN = 8, 32, 7
HALF = WIN // 2
QR, QC = 8, 14
QT = QR * QC
KR, KCOL = QR + WIN - 1, QC + WIN - 1
KEYS = KR * KCOL
BANDS = H // QR
COLS = W // QC
BAND = QR * W
GROUPS = TOKENS // BAND
TPG = BAND // QT
TILES = TOKENS // QT
KCHUNK = [(0, 5), (5, 5), (10, 4)]
CK = 5 * KCOL
MODC = 24
NEG = -30000.0
BIAS_R, BIAS_C = KR + HALF * 2, KCOL + HALF * 2
PAD_R, PAD_C = BIAS_R + QR - 1, BIAS_C + QC - 1
RPB = 2 * WIN - 1

E, FH = 8, 1024
HC = FH // 128
ST = 256
CHOICES = 2 * TOKENS
NT = (CHOICES + E * (ST - 1)) // ST
SLOTS = NT * ST
HALVES = SLOTS // 128
BLOCKS = 2 * TILES
WSCALE = 64.0
EW = KC * FH
WCH = EW // 2
MAXT = (TOKENS + ST - 1) // ST


def row_offset(r):
    return 0 if r == 0 else (-2 * HALF if r == BANDS - 1 else -HALF)


def key_col(t):
    return min(max(QC * t - HALF, 0), W - KCOL)


def split_on_act(act, w_in, hi):
    act.activation(hi, w_in, ACT.Copy, scale=WSCALE)
    return act.activation(w_in, w_in, ACT.Copy, scale=WSCALE)


def stage_a(nc, x, wqkv, bqk, bv, rpb, w1, ident, rpb_pad, rpb_cols, qk_hi, qk_lo, v_rows, bias, w1s):
    with ExitStack() as c:
        def sb(name, shape, dt):
            return c.enter_context(nc.sbuf_tensor(name, shape, dt))

        def sem(name):
            return c.enter_context(nc.semaphore(name))

        id_a = sb("a_ident", [128, 128], F32)
        w_f = sb("a_w", [128, KC, 3 * C], F32)
        w_hi = sb("a_w_hi", [128, KC, 3 * C], F16)
        w_lo = sb("a_w_lo", [128, KC, 3 * C], F16)
        b_qk = sb("a_b_qk", [128, 4], F32)
        b_v = sb("a_b_v", [QT, C], F32)
        eps = sb("a_eps", [QT, 1], F32)
        xg = sb("a_x", [QT, 2, TPG, C], F32)
        xn = sb("a_xn", [QT, 2, TPG, C], F32)
        st6 = sb("a_st6", [QT, 2, TPG, 6], F32)
        st2 = sb("a_st2", [QT, 2, TPG, 2], F32)
        sd = sb("a_sd", [QT, 2, TPG], F32)
        rs = sb("a_rs", [QT, 2, TPG], F32)
        xt_hi = sb("a_xt_hi", [128, 2, KC, BAND], F16)
        xt_lo = sb("a_xt_lo", [128, 2, KC, BAND], F16)
        o_hi = sb("a_o_hi", [128, 2, 4, BAND], F16)
        o_lo = sb("a_o_lo", [128, 2, 4, BAND], F16)
        v_f = sb("a_v_f", [QT, 2, TPG, C], F32)
        v_sb = sb("a_v", [QT, 2, TPG, NH, 2, HD], F16)
        w1_in = sb("a_w1_in", [128, 2, WCH], F32)
        pad = sb("a_pad", [NH, PAD_R, PAD_C], F32)
        ps_t = c.enter_context(nc.psum_tensor("a_ps_t", [128, KC, 512], F32))
        ps_q = c.enter_context(nc.psum_tensor("a_ps_q", [128, 4, 512], F32))
        ps_v = c.enter_context(nc.psum_tensor("a_ps_v", [128, 2, 512], F32))

        consts = sem("a_consts")
        ident_in = sem("a_ident_in")
        scaled = sem("a_scaled")
        w_ok = sem("a_w_ok")
        b_ok = sem("a_b_ok")
        x_in = [sem(f"a_x_in{i}") for i in range(2)]
        x_used = sem("a_x_used")
        stat = sem("a_stat")
        var_ok = sem("a_var_ok")
        sd_ok = sem("a_sd_ok")
        xn_ok = sem("a_xn_ok")
        t_ok = sem("a_t_ok")
        hi_ok = sem("a_hi_ok")
        xt_ok = sem("a_xt_ok")
        q_ok = sem("a_q_ok")
        qh_ok = sem("a_qh_ok")
        qk_out = sem("a_qk_out")
        v_ok = sem("a_v_ok")
        v_read = sem("a_v_read")
        vf_ok = sem("a_vf_ok")
        vh_ok = sem("a_vh_ok")
        v_out = sem("a_v_out")
        v_used = sem("a_v_used")
        w1_ld = [sem(f"a_w1_ld{i}") for i in range(2)]
        w1_hi = sem("a_w1_hi")
        w1_free = sem("a_w1_free")
        stored_hi = [sem(f"a_stored_hi{i}") for i in range(2)]
        stored_lo = [sem(f"a_stored_lo{i}") for i in range(2)]
        stored_v = [sem(f"a_stored_v{i}") for i in range(2)]
        pad_step = sem("a_pad_step")
        pad_in = sem("a_pad_in")

        def by_row(t2):
            return t2.rearrange("p (r t w) -> p r t w", r=QR, t=COLS)

        def by_tile(buf, s, m):
            return buf[:, s, m, :].rearrange("p (t r w) -> p r t w", r=QR, t=COLS) if m < 2 else by_row(buf[:, s, m, :])

        def w1_part(n, e, s):
            return w1s[:, bass.ds(e, 1), n, s * WCH:(s + 1) * WCH].rearrange("p a n -> p (a n)")

        with nc.Block() as block:

            @block.sync
            def _(sp):
                def load(s, tok):
                    sp.dma_start(xg[:, s], x[bass.ds(tok, BAND), :].rearrange("(t p) c -> p t c", p=QT)
                                 ).then_inc(x_in[s], 16)

                def load_w1(s, e):
                    sp.dma_start(w1_in[:, s], w1[:, bass.ds(e, 1), s * WCH:(s + 1) * WCH
                                                 ].rearrange("p a n -> p (a n)")).then_inc(w1_ld[s], 16)

                def step(s, tok, e, left):
                    if left >= 1:
                        sp.wait_ge(x_used, s + 1)
                    if left >= 3:
                        load(1 - s, tok + 3 * BAND)
                    sp.wait_ge(w1_free, s + 1)
                    if e is not None:
                        load_w1(s, e)
                    sp.wait_ge(qk_out, s + 1)
                    sp.dma_start(qk_hi[:, :, bass.ds(tok, BAND)], o_hi[:, s]).then_inc(stored_hi[s], 16)
                    sp.dma_start(qk_lo[:, :, bass.ds(tok, BAND)], o_lo[:, s]).then_inc(stored_lo[s], 16)
                    sp.wait_ge(v_out, s + 1)
                    sp.dma_start(v_rows[bass.ds(tok, BAND), :].rearrange("(t p) c -> p t c", p=QT),
                                 v_sb[:, s].rearrange("p t h a d -> p t (h a d)")).then_inc(stored_v[s], 16)

                load(0, 0)
                sp.dma_start(id_a[:, :], ident).then_inc(ident_in, 16)
                sp.dma_start(w_f[:, :, :], wqkv).then_inc(consts, 16)
                sp.dma_start(b_qk[:, :], bqk).then_inc(consts, 16)
                sp.dma_start(b_v[:, :], bv.to_broadcast([QT, C])).then_inc(consts, 16)
                load(1, BAND)
                for s in range(2):
                    load_w1(s, 0)
                sp.wait_ge(x_used, 1)
                sp.sem_inc(x_used, -1)
                load(0, 2 * BAND)
                for s in range(2):
                    sp.wait_ge(w1_free, s + 1)
                    load_w1(s, 1)
                sp.sem_inc(w1_free, -2)
                with sp.Fori(0, GROUPS // 2 - 2) as i:
                    for s in range(2):
                        step(s, (2 * i + s) * BAND, i + 2, 3)
                    for q in (x_used, w1_free, qk_out, v_out):
                        sp.sem_inc(q, -2)
                step(0, (GROUPS - 4) * BAND, E - 1, 3)
                step(1, (GROUPS - 3) * BAND, E - 1, 2)
                for q in (x_used, w1_free, qk_out, v_out):
                    sp.sem_inc(q, -2)
                step(0, (GROUPS - 2) * BAND, None, 1)
                step(1, (GROUPS - 1) * BAND, None, 0)

            @block.vector
            def _(dve):
                dve.memset(eps[:, :], 1e-6)
                dve.sem_inc(stored_lo[0], 16)
                dve.sem_inc(stored_lo[1], 16)
                dve.sem_inc(v_used, 2)

                def normalise(s):
                    dve.wait_ge(x_in[s], 16)
                    dve.sem_inc(x_in[s], -16)
                    for t in range(TPG):
                        last = dve.bn_stats(st6[:, s, t, :], xg[:, s, t, :])
                    last.then_inc(stat, 1)
                    dve.wait_ge(stat, 1)
                    for t in range(TPG):
                        last = dve.bn_aggr(st2[:, s, t, :], st6[:, s, t, :])
                    last.then_inc(var_ok, 1)

                def scale(s):
                    dve.wait_ge(sd_ok, 1)
                    dve.sem_inc(sd_ok, -1)
                    dve.reciprocal(rs[:, s, :], sd[:, s, :]).then_inc(stat, 1)
                    dve.wait_ge(stat, 2)
                    dve.sem_inc(stat, -2)
                    for t in range(TPG):
                        last = dve.tensor_scalar(xn[:, s, t, :], xg[:, s, t, :], st2[:, s, t, 0:1], rs[:, s, t:t + 1],
                                                 ALU.subtract, ALU.mult)
                    last.then_inc(xn_ok, 1)

                def low_half(s):
                    dve.wait_ge(hi_ok, 1)
                    dve.sem_inc(hi_ok, -1)
                    dve.tensor_tensor(xt_lo[:, s], ps_t[:, :, 0:BAND], xt_hi[:, s], ALU.subtract).then_inc(xt_ok, 1)

                def step(s, last):
                    if not last:
                        normalise(1 - s)
                    dve.wait_ge(stored_lo[s], 16)
                    dve.sem_inc(stored_lo[s], -16)
                    for m in range(4):
                        dve.wait_ge(qh_ok, m + 1)
                        b = b_qk[:, m:m + 1]
                        if m < 2:
                            for t in range(COLS):
                                low = dve.scalar_tensor_tensor(
                                    o_lo[:, s, m, t * QT:(t + 1) * QT].rearrange("p (r w) -> p r w", r=QR),
                                    by_row(ps_q[:, m, 0:BAND])[:, :, t, :], b,
                                    o_hi[:, s, m, t * QT:(t + 1) * QT].rearrange("p (r w) -> p r w", r=QR),
                                    ALU.add, ALU.subtract)
                        else:
                            low = dve.scalar_tensor_tensor(o_lo[:, s, m, :], ps_q[:, m, 0:BAND], b, o_hi[:, s, m, :],
                                                           ALU.add, ALU.subtract)
                        if m == 0 and not last:
                            scale(1 - s)
                        if m == 1 and not last:
                            low.then_inc(x_used, 1)
                    low.then_inc(qk_out, 1)
                    dve.sem_inc(qh_ok, -4)
                    if not last:
                        low_half(1 - s)
                    dve.wait_ge(v_used, 1)
                    dve.sem_inc(v_used, -1)
                    for t in range(0, TPG, 2):
                        dve.wait_ge(v_ok, t // 2 + 1)
                        add = dve.tensor_tensor(v_f[:, s, t:t + 2, :],
                                                ps_v[0:QT, t // 2, :].rearrange("p (t c) -> p t c", t=2),
                                                b_v[:, :].rearrange("p (a c) -> p a c", a=1).to_broadcast([QT, 2, C]),
                                                ALU.add)
                        add.then_inc(vf_ok if t else v_read, 1)
                    dve.sem_inc(v_ok, -2)

                normalise(0)
                dve.wait_ge(consts, 48)
                dve.tensor_scalar(w_f[:, :, 0:C], w_f[:, :, 0:C], HD ** -0.5, None, ALU.mult).then_inc(scaled, 1)
                dve.tensor_scalar(b_qk[:, 0:2], b_qk[:, 0:2], HD ** -0.5, None, ALU.mult).then_inc(b_ok, 1)
                scale(0)
                dve.wait_ge(scaled, 1)
                dve.tensor_copy(w_hi[:, 0], w_f[:, 0]).then_inc(x_used, 1)
                dve.tensor_copy(w_hi[:, 1], w_f[:, 1]).then_inc(scaled, 1)
                dve.wait_ge(scaled, 2)
                dve.tensor_tensor(w_lo[:, :, :], w_f[:, :, :], w_hi[:, :, :], ALU.subtract).then_inc(w_ok, 1)
                low_half(0)
                with dve.Fori(0, GROUPS // 2 - 1):
                    for s in range(2):
                        step(s, False)
                step(0, False)
                step(1, True)
                for s in range(2):
                    dve.wait_ge(stored_lo[s], 16)

            @block.scalar
            def _(act):
                for s in range(2):
                    act.sem_inc(stored_hi[s], 16)
                    act.sem_inc(stored_v[s], 16)

                def roots(s):
                    act.wait_ge(var_ok, 1)
                    act.sem_inc(var_ok, -1)
                    act.activation(sd[:, s, :], st2[:, s, :, 1], ACT.Sqrt, bias=eps[:, :]).then_inc(sd_ok, 1)

                def high_half(s):
                    act.wait_ge(t_ok, 1)
                    act.sem_inc(t_ok, -1)
                    act.copy(xt_hi[:, s], ps_t[:, :, 0:BAND]).then_inc(hi_ok, 1)

                def split_w1(s, e):
                    act.wait_ge(w1_ld[s], 16)
                    act.sem_inc(w1_ld[s], -16)
                    split_on_act(act, w1_in[:, s], w1_part(0, e, s)).then_inc(w1_hi, 1)

                def step(s, e, last):
                    if not last:
                        roots(1 - s)
                    act.wait_ge(stored_hi[s], 16)
                    act.sem_inc(stored_hi[s], -16)
                    for m in range(4):
                        act.wait_ge(q_ok, m + 1)
                        act.activation(by_tile(o_hi, s, m), by_row(ps_q[:, m, 0:BAND]), ACT.Identity,
                                       bias=b_qk[:, m:m + 1]).then_inc(qh_ok, 1)
                    act.sem_inc(q_ok, -4)
                    if not last:
                        high_half(1 - s)
                    split_w1(s, e)
                    act.wait_ge(stored_v[s], 16)
                    act.sem_inc(stored_v[s], -16)
                    act.wait_ge(vf_ok, 1)
                    act.sem_inc(vf_ok, -1)
                    act.copy(v_sb[:, s, :, :, 0, :], v_f[:, s].rearrange("p t (h d) -> p t h d", h=NH)
                             ).then_inc(vh_ok, 1)

                roots(0)
                high_half(0)
                for s in range(2):
                    split_w1(s, 0)
                act.wait_ge(b_ok, 1)
                with act.Fori(0, GROUPS // 2 - 1) as i:
                    for s in range(2):
                        step(s, i + 1, False)
                step(0, E - 1, False)
                step(1, E - 1, True)
                for s in range(2):
                    act.wait_ge(stored_hi[s], 16)
                    act.wait_ge(stored_v[s], 16)

            @block.gpsimd
            def _(pool):
                def split_w1(s, e, first):
                    pool.wait_ge(w1_hi, 1)
                    pool.sem_inc(w1_hi, -1)
                    for a, b in ((0, 128), (128, WCH)):
                        low = pool.tensor_tensor(w1_part(1, e, s)[:, a:b], w1_in[:, s, a:b], w1_part(0, e, s)[:, a:b],
                                                 ALU.subtract)
                        if a == 0 and not first:
                            low.then_inc(v_used, 1)
                    low.then_inc(w1_free, 1)

                pool.memset(pad[:, :, :], 0.0).then_inc(pad_step, 1)
                pool.wait_ge(pad_step, 1)
                pool.dma_start(pad[:, QR - 1:QR - 1 + RPB, QC - 1:QC - 1 + RPB], rpb).then_inc(pad_in, 16)
                pool.wait_ge(pad_in, 16)
                pool.dma_start(rpb_pad, pad[:, :, :]).then_inc(pad_in, 16)
                pool.wait_ge(pad_in, 32)
                for j in range(QC):
                    pool.dma_start(rpb_cols[j], rpb_pad[:, :, QC - 1 - j:QC - 1 - j + BIAS_C]).then_inc(pad_in, 16)
                for s in range(2):
                    split_w1(s, 0, True)
                pool.wait_ge(pad_in, 32 + 16 * QC)
                for i in range(QR):
                    pool.dma_start(bias[i * QC:(i + 1) * QC], rpb_cols[:, :, QR - 1 - i:QR - 1 - i + BIAS_R, :]
                                   ).then_inc(pad_in, 16)
                with pool.Fori(0, GROUPS // 2) as i:
                    for s in range(2):
                        pool.wait_ge(vh_ok, 1)
                        pool.sem_inc(vh_ok, -1)
                        pool.tensor_tensor(v_sb[:, s, :, :, 1, :], v_f[:, s].rearrange("p t (h d) -> p t h d", h=NH),
                                           v_sb[:, s, :, :, 0, :], ALU.subtract).then_inc(v_out, 1)
                        split_w1(s, i + 1, False)
                pool.wait_ge(pad_in, 32 + 16 * QC + 16 * QR)

            @block.tensor
            def _(pe):
                pe.wait_ge(ident_in, 16)
                parts = ((w_hi, xt_hi), (w_hi, xt_lo), (w_lo, xt_hi))

                def transposes(s):
                    pe.wait_ge(xn_ok, 1)
                    pe.sem_inc(xn_ok, -1)
                    for k in range(KC):
                        for t in range(TPG):
                            last = pe.transpose(ps_t[:, k, t * QT:(t + 1) * QT], xn[:, s, t, k * 128:(k + 1) * 128],
                                                id_a[0:QT, 0:QT])
                    last.then_inc(t_ok, 1)

                def step(s, last):
                    pe.wait_ge(xt_ok, 1)
                    pe.sem_inc(xt_ok, -1)
                    for m in range(4):
                        for n in range(3 * KC):
                            (w, xx), k = parts[n % 3], n // 3
                            mm = pe.matmul(ps_q[:, m, 0:BAND], w[:, k, m * 128:(m + 1) * 128], xx[:, s, k, :],
                                           start=n == 0, stop=n == 3 * KC - 1)
                        mm.then_inc(q_ok, 1)
                    if not last:
                        transposes(1 - s)
                    for t in range(TPG):
                        if last and t % 2 == 0:
                            pe.wait_ge(v_read, GROUPS - 1 + t // 2)
                        for n in range(3 * KC):
                            (w, xx), k = parts[n % 3], n // 3
                            mm = pe.matmul(ps_v[0:QT, t // 2, (t % 2) * C:(t % 2 + 1) * C],
                                           xx[:, s, k, t * QT:(t + 1) * QT], w[:, k, 2 * C:3 * C],
                                           start=n == 0, stop=n == 3 * KC - 1)
                        if t % 2:
                            mm.then_inc(v_ok, 1)

                transposes(0)
                pe.wait_ge(w_ok, 1)
                with pe.Fori(0, GROUPS // 2 - 1):
                    for s in range(2):
                        step(s, False)
                step(0, False)
                step(1, True)




def stage_b(nc, qk_hi, qk_lo, v_rows, bias, q_mask, k_mask, ident16, attn):
    with ExitStack() as c:
        def sb(name, shape, dt):
            return c.enter_context(nc.sbuf_tensor(name, shape, dt))

        def sem(name):
            return c.enter_context(nc.semaphore(name))

        id_b = sb("b_ident", [128, 128], F16)
        q_st = sb("b_q", [128, 2, NH, BAND], F16)
        k_st = sb("b_k", [128, 2, NH, KR * W], F16)
        v_st = sb("b_v", [CK, 4, 3, NH * 2 * HD], F16)
        s_sb = sb("b_s", [QT, 8, KEYS], F32)
        p16 = sb("b_p16", [QT, 8, 2 * KEYS + 48], F16)
        pt_sb = sb("b_pt", [CK, 4, 6, 128], F16)
        neg_max = sb("b_neg_max", [QT, 4, NH], F32)
        total = sb("b_total", [QT, 4, NH], F32)
        inv = sb("b_inv", [QT, 2, NH], F32)
        o_sb = sb("b_o", [QT, 2, C], F32)
        ps_s = c.enter_context(nc.psum_tensor("b_ps_s", [128, 4, 512], F32))
        ps_p = c.enter_context(nc.psum_tensor("b_ps_p", [128, 2, 1024], F16))
        ps_o = c.enter_context(nc.psum_tensor("b_ps_o", [128, 2, 512], F32))

        ident_in = sem("b_ident_in")
        q_mask_in = sem("b_q_mask_in")
        band_in = [sem(f"b_band_in{i}") for i in range(2)]
        v_in = [sem(f"b_v_in{i}") for i in range(4)]
        clear = sem("b_clear")
        s_ok = sem("b_s_ok")
        m_ok = sem("b_m_ok")
        p_ok = sem("b_p_ok")
        hi_ok = sem("b_hi_ok")
        lo_ok = sem("b_lo_ok")
        t_ok_act = sem("b_t_ok_act")
        t_ok_dve = sem("b_t_ok_dve")
        pt_ok_act = sem("b_pt_ok_act")
        pt_ok_dve = sem("b_pt_ok_dve")
        o_ok = sem("b_o_ok")
        norm = sem("b_norm")
        o_out = sem("b_o_out")
        qk_used = sem("b_qk_used")
        stored = [sem(f"b_stored{i}") for i in range(2)]

        grid = attn.rearrange("(b h w) c -> b h w c", b=B, h=H)
        v_grid = v_rows.rearrange("(b h w) c -> b h w c", b=B, h=H)
        TP = 2 * COLS
        NHT = TP * NH
        CAST_LAG, READ_LAG, T_LAG, EVAC_LAG, V_LAG = 2, 6, 8, 8, 10

        def on_dve(j):
            return j % 4 == 3

        def earlier(k, lag, first):
            return k - lag if k >= lag else (None if first else k - lag + NHT)

        with nc.Block() as block:

            @block.sync
            def _(sp):
                sp.dma_start(id_b[:, :], ident16).then_inc(ident_in, 16)
                for s in range(2):
                    sp.dma_start(q_st[96:128, s], q_mask.rearrange("p (a n) -> p a n", a=1).to_broadcast([32, NH, BAND])
                                 ).then_inc(q_mask_in, 16)

                def load_band(s, r, r0):
                    cls = 0 if isinstance(r, int) and r == 0 else (2 if isinstance(r, int) and r == BANDS - 1 else 1)
                    q0 = s * H * W + r * BAND
                    k0 = s * H * W + r0 * W
                    for part, src in enumerate((qk_hi, qk_hi, qk_lo)):
                        for m in range(2):
                            sp.dma_start(q_st[32 * part:32 * part + 32, s, 4 * m:4 * m + 4, :],
                                         src[:, m, bass.ds(q0, BAND)].rearrange("(h d) n -> d h n", d=HD)
                                         ).then_inc(band_in[s], 16)
                    for part, src in enumerate((qk_hi, qk_lo, qk_hi)):
                        for m in range(2):
                            sp.dma_start(k_st[32 * part:32 * part + 32, s, 4 * m:4 * m + 4, :],
                                         src[:, 2 + m, bass.ds(k0, KR * W)].rearrange("(h d) n -> d h n", d=HD)
                                         ).then_inc(band_in[s], 16)
                    sp.dma_start(k_st[96:128, s], k_mask[cls].rearrange("p (a n) -> p a n", a=1
                                                                      ).to_broadcast([32, NH, KR * W])
                                 ).then_inc(band_in[s], 16)

                def load_v(s, t, r0):
                    for j, (a, n) in enumerate(KCHUNK):
                        sp.dma_start(v_st[0:n * KCOL, t, j, :],
                                     v_grid[s, bass.ds(r0 + a, n), key_col(t):key_col(t) + KCOL, :]
                                     ).then_inc(v_in[t], 16)

                def pair(r, r0, r_next, r0_next):
                    for s in range(2):
                        for t in range(COLS):
                            n = s * COLS + t
                            sp.wait_ge(o_out, n + 1)
                            sp.dma_start(grid[s, bass.ds(r * QR, QR), t * QC:(t + 1) * QC, :], o_sb[:, n % 2, :]
                                         ).then_inc(stored[n % 2], 16)
                            if s == 0:
                                load_v(1, t, r0)
                            elif r_next is not None:
                                load_v(0, t, r0_next)
                            if r_next is not None and t == COLS - 2:
                                sp.wait_ge(qk_used, s + 1)
                                load_band(s, r_next, r0_next)
                    if r_next is not None:
                        sp.sem_inc(qk_used, -2)
                    sp.sem_inc(o_out, -TP)

                load_band(0, 0, 0)
                for t in range(COLS):
                    load_v(0, t, 0)

                load_band(1, 0, 0)

                pair(0, 0, 1, QR - HALF)
                with sp.Fori(1, BANDS - 2) as r:
                    pair(r, r * QR - HALF, r + 1, (r + 1) * QR - HALF)
                pair(BANDS - 2, (BANDS - 2) * QR - HALF, BANDS - 1, H - KR)
                pair(BANDS - 1, H - KR, None, None)

            @block.tensor
            def _(pe):
                pe.wait_ge(ident_in, 16)
                pe.wait_ge(clear, 1)
                pe.wait_ge(q_mask_in, 32)

                def scores(j):
                    s, t, h = j // (COLS * NH), j // NH % COLS, j % NH
                    if j % (COLS * NH) == 0:
                        pe.wait_ge(band_in[s], 13 * 16)
                        pe.sem_inc(band_in[s], -13 * 16)
                    q = q_st[:, s, h, t * QT:(t + 1) * QT]
                    k = k_st[:, s, h, :].rearrange("p (r w) -> p r w", w=W)[:, :, key_col(t):key_col(t) + KCOL]
                    mm = pe.matmul(ps_s[0:QT, j % 4, 0:KEYS], q, k, start=True, stop=True).then_inc(s_ok, 1)
                    if j % (COLS * NH) == COLS * NH - 1:
                        return s
                    return None

                def transposes(j):
                    for half in range(2):
                        for n, (a, _) in enumerate(KCHUNK):
                            m = 3 * half + n
                            last = pe.transpose(ps_p[:, j % 2, m * QT:(m + 1) * QT],
                                                p16[:, j % 8, half * KEYS + a * KCOL:][:, 0:128], id_b[0:QT, 0:QT])
                    last.then_inc(t_ok_dve if on_dve(j) else t_ok_act, 1)

                def values(j, signal=None):
                    n, h = j // NH, j % NH
                    t = n % COLS
                    if h == 0:
                        pe.wait_ge(v_in[t], 48)
                        pe.sem_inc(v_in[t], -48)
                    terms = [(m, half, part) for m in range(3) for half, part in ((0, 0), (0, 1), (1, 0))]
                    for i, (m, half, part) in enumerate(terms):
                        keys, at = KCHUNK[m][1] * KCOL, (2 * h + part) * HD
                        last = pe.matmul(ps_o[:, n % 2, h * HD:(h + 1) * HD], pt_sb[0:keys, j % 4, 3 * half + m, :],
                                         v_st[0:keys, t, m, at:at + HD], start=i == 0, stop=i == len(terms) - 1)
                        if i == 0 and signal is not None:
                            last.then_inc(signal, 1)
                    if h == NH - 1:
                        last.then_inc(o_ok, 1)

                def pair(first, last):
                    used = {q: 0 for q in (lo_ok, pt_ok_act, pt_ok_dve)}

                    def take(q):
                        used[q] += 1
                        pe.wait_ge(q, used[q])

                    for k in range(NHT + (V_LAG if last else 0)):
                        lo, tr, va = (earlier(k, lag, first) for lag in (READ_LAG, T_LAG, V_LAG))
                        if first and k == 4:
                            pe.wait_ge(lo_ok, 1)
                        if lo is not None and lo < NHT:
                            take(lo_ok)
                        band_done = scores(k) if k < NHT else None
                        if va is not None:
                            take(pt_ok_dve if on_dve(va) else pt_ok_act)
                        if tr is not None and tr < NHT:
                            transposes(tr)
                        if va is not None:
                            values(va, qk_used if band_done is not None else None)
                    for q, n in used.items():
                        pe.sem_inc(q, -n)

                pair(True, False)
                with pe.Fori(1, BANDS - 1):
                    pair(False, False)
                pair(False, True)

            @block.vector
            def _(dve):
                dve.memset(pt_sb[:, :, :, :].rearrange("p a m q -> p (a m q)").bitcast(F32), 0.0)
                dve.memset(p16[:, :, :].rearrange("p a n -> p (a n)").bitcast(F32), 0.0).then_inc(clear, 1)
                for s in range(2):
                    dve.sem_inc(stored[s], 16)

                def bias_and_max(j, off):
                    n, h, t = j // NH, j % NH, j // NH % COLS
                    y, xx = off + WIN - 1, key_col(t) - t * QC + WIN - 1
                    dve.wait_ge(s_ok, j + 1)
                    dve.tensor_tensor_reduce(
                        out=s_sb[:, j % 8, :].rearrange("p (r w) -> p r w", w=KCOL),
                        in0=ps_s[0:QT, j % 4, 0:KEYS].rearrange("p (r w) -> p r w", w=KCOL),
                        in1=bias[:, h, y:y + KR, xx:xx + KCOL], scale=-1.0, scalar=3.0e38, op0=ALU.add, op1=ALU.min,
                        accum_out=neg_max[:, n % 4, h:h + 1]).then_inc(m_ok, 1)

                def pair(off, first, last):
                    used = {q: 0 for q in (p_ok, t_ok_dve, o_ok, norm)}

                    def take(q):
                        used[q] += 1
                        dve.wait_ge(q, used[q])

                    def evacuate(j):
                        take(t_ok_dve)
                        dve.tensor_copy(pt_sb[:, j % 4, :, :].bitcast(I32)[:, :, 0:QT // 2],
                                        ps_p[0:CK, j % 2, 0:6 * QT].bitcast(I32).rearrange("p (m q) -> p m q", m=6)).then_inc(pt_ok_dve, 1)

                    def cast(j):
                        take(p_ok)
                        dve.tensor_copy(p16[:, j % 8, 0:KEYS], s_sb[:, j % 8, :]).then_inc(hi_ok, 1)

                    def normalise(n):
                        take(o_ok)
                        dve.wait_ge(stored[n % 2], 16)
                        dve.sem_inc(stored[n % 2], -16)
                        take(norm)
                        dve.tensor_tensor(o_sb[:, n % 2, :].rearrange("p (h d) -> p h d", h=NH),
                                          ps_o[0:QT, n % 2, 0:C].rearrange("p (h d) -> p h d", h=NH),
                                          inv[:, n % 2, :].rearrange("p (h a) -> p h a", a=1).to_broadcast([QT, NH, HD]),
                                          ALU.mult).then_inc(o_out, 1)

                    for k in range(NHT + (NH + 3 if last else 0)):
                        ev, ca = earlier(k, EVAC_LAG, first), earlier(k, CAST_LAG, first)
                        if k < NHT:
                            bias_and_max(k, off)
                        if ev is not None and ev < NHT and on_dve(ev):
                            evacuate(ev)
                        if ca is not None and ca < NHT:
                            cast(ca)
                        summed = earlier(k, 2 * NH, first)
                        if summed is not None and summed % NH == 0 and summed < NHT:
                            n = summed // NH
                            dve.reciprocal(inv[:, n % 2, :], total[:, n % 4, :]).then_inc(norm, 1)
                        done = earlier(k, NH + V_LAG, first)
                        if done is not None and done % NH == 0 and done < NHT:
                            normalise(done // NH)
                    used[s_ok] = NHT
                    for q, n in used.items():
                        dve.sem_inc(q, -n)

                pair(row_offset(0), True, False)
                with dve.Fori(1, BANDS - 1):
                    pair(row_offset(1), False, False)
                pair(row_offset(BANDS - 1), False, True)
                for s in range(2):
                    dve.wait_ge(stored[s], 16)

            @block.scalar
            def _(act):
                def exponential(j):
                    n, h = j // NH, j % NH
                    act.wait_ge(m_ok, j + 1)
                    act.activation(s_sb[:, j % 8, :], s_sb[:, j % 8, :], ACT.Exp, bias=neg_max[:, n % 4, h:h + 1],
                                   scale=-1.0, accum_out=total[:, n % 4, h:h + 1]).then_inc(p_ok, 1)

                def pair(first, last):
                    used = 0
                    for k in range(NHT + (EVAC_LAG if last else 0)):
                        ev = earlier(k, EVAC_LAG, first)
                        if ev is not None and not on_dve(ev):
                            used += 1
                            act.wait_ge(t_ok_act, used)
                            act.copy(pt_sb[:, ev % 4, :, :].bitcast(I32)[:, :, 0:QT // 2],
                                     ps_p[0:CK, ev % 2, 0:6 * QT].bitcast(I32).rearrange("p (m q) -> p m q", m=6)).then_inc(pt_ok_act, 1)
                        if k < NHT:
                            exponential(k)
                    act.sem_inc(m_ok, -NHT)
                    act.sem_inc(t_ok_act, -used)

                pair(True, False)
                with act.Fori(1, BANDS - 1):
                    pair(False, False)
                pair(False, True)

            @block.gpsimd
            def _(pool):
                with pool.Fori(0, BANDS):
                    for j in range(NHT):
                        pool.wait_ge(hi_ok, j + 1)
                        pool.tensor_tensor(p16[:, j % 8, KEYS:2 * KEYS], s_sb[:, j % 8, :], p16[:, j % 8, 0:KEYS], ALU.subtract
                                           ).then_inc(lo_ok, 1)
                    pool.sem_inc(hi_ok, -NHT)


def stage_c(nc, x, attn, wproj, bproj, wg, bg, ident, x1_dram, xs_dram, logits):
    with ExitStack() as c:
        def sb(name, shape, dt):
            return c.enter_context(nc.sbuf_tensor(name, shape, dt))

        def sem(name):
            return c.enter_context(nc.semaphore(name))

        id_c = sb("c_ident", [128, 128], F32)
        w_p = sb("c_w_p", [128, KC, C], F32)
        w_g = sb("c_w_g", [128, KC, E], F32)
        b_p = sb("c_b_p", [QT, C], F32)
        b_g = sb("c_b_g", [QT, E], F32)
        eps = sb("c_eps", [QT, 1], F32)
        a_sb = sb("c_a", [QT, 2, TPG, C], F32)
        x_sb = sb("c_x", [QT, 2, TPG, C], F32)
        x1 = sb("c_x1", [QT, 2, TPG, C], F32)
        xn = sb("c_xn", [QT, 2, TPG, C], F32)
        xs = sb("c_xs", [QT, 2, TPG, 2, C], F16)
        at = sb("c_at", [128, KC, BAND], F32)
        xt = sb("c_xt", [128, KC, BAND], F32)
        st6 = sb("c_st6", [QT, TPG, 6], F32)
        st2 = sb("c_st2", [QT, 2, TPG, 2], F32)
        sd = sb("c_sd", [QT, 2, TPG], F32)
        rs = sb("c_rs", [QT, 2, TPG], F32)
        ps_a = c.enter_context(nc.psum_tensor("c_ps_a", [128, KC, 512], F32))
        ps_p = c.enter_context(nc.psum_tensor("c_ps_p", [128, 2, 512], F32))
        ps_x = c.enter_context(nc.psum_tensor("c_ps_x", [128, KC, 512], F32))
        ps_g = c.enter_context(nc.psum_tensor("c_ps_g", [128, 2, 512], F32))

        w_in = sem("c_w_in")
        bp_in = sem("c_bp_in")
        bg_in = sem("c_bg_in")
        eps_ok = sem("c_eps_ok")
        a_in = [sem(f"c_a_in{i}") for i in range(2)]
        x_in = [sem(f"c_x_in{i}") for i in range(2)]
        a_tr = sem("c_a_tr")
        a_ev = sem("c_a_ev")
        xb_ok = sem("c_xb_ok")
        p_ok = sem("c_p_ok")
        stat = sem("c_stat")
        var_ok = sem("c_var_ok")
        sd_ok = sem("c_sd_ok")
        xn_ok = sem("c_xn_ok")
        x_tr = sem("c_x_tr")
        x_ev = sem("c_x_ev")
        hi_ok = sem("c_hi_ok")
        out_ok = sem("c_out_ok")
        g_ok = sem("c_g_ok")
        st_x1 = [sem(f"c_st_x1{i}") for i in range(2)]
        st_xs = [sem(f"c_st_xs{i}") for i in range(2)]

        def rows(t, tok):
            return t[bass.ds(tok, BAND), :].rearrange("(t p) c -> p t c", p=QT)

        with nc.Block() as block:

            @block.sync
            def _(sp):
                def load(s, tok):
                    sp.dma_start(a_sb[:, s], rows(attn, tok)).then_inc(a_in[s], 16)
                    sp.dma_start(x_sb[:, s], rows(x, tok)).then_inc(x_in[s], 16)

                def step(s, tok, last):
                    sp.wait_ge(out_ok, s + 1)
                    sp.dma_start(rows(x1_dram, tok), x1[:, s]).then_inc(st_x1[s], 16)
                    sp.dma_start(rows(xs_dram, tok), xs[:, s].rearrange("p t a c -> p t (a c)")).then_inc(st_xs[s], 16)
                    if not last:
                        load(s, tok + 2 * BAND)

                load(0, 0)
                for dst, src in ((w_p[:, :, :], wproj), (w_g[:, :, :], wg), (id_c[:, :], ident)):
                    sp.dma_start(dst, src).then_inc(w_in, 16)
                sp.dma_start(b_p[:, :], bproj.to_broadcast([QT, C])).then_inc(bp_in, 16)
                sp.dma_start(b_g[:, :], bg.to_broadcast([QT, E])).then_inc(bg_in, 16)
                load(1, BAND)
                with sp.Fori(0, GROUPS // 2 - 1) as i:
                    for s in range(2):
                        step(s, (2 * i + s) * BAND, False)
                    sp.sem_inc(out_ok, -2)
                for s in range(2):
                    step(s, (GROUPS - 2 + s) * BAND, True)

            @block.tensor
            def _(pe):
                pe.wait_ge(w_in, 48)

                def transposes(dst, src, done):
                    for k in range(KC):
                        for t in range(TPG):
                            last = pe.transpose(dst[:, k, t * QT:(t + 1) * QT], src[:, t, k * 128:(k + 1) * 128],
                                                id_c[0:QT, 0:QT])
                    last.then_inc(done, 1)

                def turn_attention(s):
                    pe.wait_ge(a_in[s], 16)
                    pe.sem_inc(a_in[s], -16)
                    transposes(ps_a, a_sb[:, s], a_tr)

                def project():
                    pe.wait_ge(a_ev, 1)
                    pe.sem_inc(a_ev, -1)
                    for t in range(TPG):
                        for k in range(KC):
                            last = pe.matmul(ps_p[0:QT, t // 2, (t % 2) * C:(t % 2 + 1) * C],
                                             at[:, k, t * QT:(t + 1) * QT], w_p[:, k, :], start=k == 0, stop=k == KC - 1)
                    last.then_inc(p_ok, 1)

                def turn_xn(s):
                    pe.wait_ge(xn_ok, 1)
                    pe.sem_inc(xn_ok, -1)
                    transposes(ps_x, xn[:, s], x_tr)

                def gate(s):
                    pe.wait_ge(x_ev, 1)
                    pe.sem_inc(x_ev, -1)
                    for t in range(TPG):
                        for k in range(KC):
                            last = pe.matmul(ps_g[0:QT, s, t * E:(t + 1) * E], xt[:, k, t * QT:(t + 1) * QT], w_g[:, k, :],
                                             start=k == 0, stop=k == KC - 1)
                    last.then_inc(g_ok, 1)

                def step(s, last):
                    if not last:
                        turn_attention(1 - s)
                    turn_xn(s)
                    if not last:
                        project()
                    gate(s)

                turn_attention(0)
                project()
                with pe.Fori(0, GROUPS // 2 - 1):
                    for s in range(2):
                        step(s, False)
                step(0, False)
                step(1, True)

            @block.scalar
            def _(act):
                for s in range(2):
                    act.sem_inc(st_xs[s], 16)
                act.wait_ge(eps_ok, 1)

                def take(dst, src, ready, done):
                    act.wait_ge(ready, 1)
                    act.sem_inc(ready, -1)
                    act.copy(dst, src).then_inc(done, 1)

                def roots(s):
                    act.wait_ge(var_ok, 1)
                    act.sem_inc(var_ok, -1)
                    act.activation(sd[:, s, :], st2[:, s, :, 1], ACT.Sqrt, bias=eps[:, :]).then_inc(sd_ok, 1)

                def high_half(s):
                    act.wait_ge(st_xs[s], 16)
                    act.sem_inc(st_xs[s], -16)
                    act.copy(xs[:, s, :, 0, :], xn[:, s]).then_inc(hi_ok, 1)

                def step(s, last):
                    if not last:
                        take(at[:, :, :], ps_a[:, :, 0:BAND], a_tr, a_ev)
                    take(xt[:, :, :], ps_x[:, :, 0:BAND], x_tr, x_ev)
                    high_half(s)
                    if not last:
                        roots(1 - s)

                take(at[:, :, :], ps_a[:, :, 0:BAND], a_tr, a_ev)
                roots(0)
                with act.Fori(0, GROUPS // 2 - 1):
                    for s in range(2):
                        step(s, False)
                step(0, False)
                step(1, True)
                for s in range(2):
                    act.wait_ge(st_xs[s], 16)

            @block.gpsimd
            def _(pool):
                pool.wait_ge(bp_in, 16)

                def add_bias(s):
                    pool.wait_ge(x_in[s], 16)
                    pool.sem_inc(x_in[s], -16)
                    pool.tensor_tensor(x_sb[:, s], x_sb[:, s], b_p[:, :].rearrange("p (a c) -> p a c", a=1
                                                                                 ).to_broadcast([QT, TPG, C]), ALU.add
                                       ).then_inc(xb_ok, 1)

                def low_half(s):
                    pool.wait_ge(hi_ok, 1)
                    pool.sem_inc(hi_ok, -1)
                    pool.tensor_tensor(xs[:, s, :, 1, :], xn[:, s], xs[:, s, :, 0, :], ALU.subtract).then_inc(out_ok, 1)

                add_bias(0)
                with pool.Fori(0, GROUPS // 2 - 1):
                    for s in range(2):
                        add_bias(1 - s)
                        low_half(s)
                add_bias(1)
                low_half(0)
                low_half(1)

            @block.vector
            def _(dve):
                dve.memset(eps[:, :], 1e-5).then_inc(eps_ok, 1)
                for s in range(2):
                    dve.sem_inc(st_x1[s], 16)
                dve.wait_ge(bg_in, 16)

                def residual_and_norm(s):
                    dve.wait_ge(xb_ok, 1)
                    dve.sem_inc(xb_ok, -1)
                    dve.wait_ge(st_x1[s], 16)
                    dve.sem_inc(st_x1[s], -16)
                    dve.wait_ge(p_ok, 1)
                    dve.sem_inc(p_ok, -1)
                    dve.tensor_tensor(x1[:, s].rearrange("p (b t) c -> p b (t c)", b=2), ps_p[0:QT, :, :],
                                      x_sb[:, s].rearrange("p (b t) c -> p b (t c)", b=2), ALU.add).then_inc(stat, 1)
                    dve.wait_ge(stat, 1)
                    for t in range(TPG):
                        last = dve.bn_stats(st6[:, t, :], x1[:, s, t, :])
                    last.then_inc(stat, 1)
                    dve.wait_ge(stat, 2)
                    for t in range(TPG):
                        last = dve.bn_aggr(st2[:, s, t, :], st6[:, t, :])
                    last.then_inc(var_ok, 1)
                    dve.wait_ge(sd_ok, 1)
                    dve.sem_inc(sd_ok, -1)
                    dve.reciprocal(rs[:, s, :], sd[:, s, :]).then_inc(stat, 1)
                    dve.wait_ge(stat, 3)
                    dve.sem_inc(stat, -3)
                    for t in range(TPG):
                        last = dve.tensor_scalar(xn[:, s, t, :], x1[:, s, t, :], st2[:, s, t, 0:1], rs[:, s, t:t + 1],
                                                 ALU.subtract, ALU.mult)
                    last.then_inc(xn_ok, 1)

                def take_logits(s, tile):
                    dve.wait_ge(g_ok, 1)
                    dve.sem_inc(g_ok, -1)
                    dve.tensor_tensor(logits[:, bass.ds(tile, TPG), :],
                                      ps_g[0:QT, s, 0:TPG * E].rearrange("p (t e) -> p t e", t=TPG),
                                      b_g[:, :].rearrange("p (a e) -> p a e", a=1).to_broadcast([QT, TPG, E]), ALU.add)

                residual_and_norm(0)
                with dve.Fori(0, GROUPS // 2 - 1) as i:
                    for s in range(2):
                        residual_and_norm(1 - s)
                        take_logits(s, (2 * i + s) * TPG)
                residual_and_norm(1)
                take_logits(0, (GROUPS - 2) * TPG)
                take_logits(1, (GROUPS - 1) * TPG)
                for s in range(2):
                    dve.wait_ge(st_x1[s], 16)


def stage_d(nc, logits, consts_f, tri, iota_hi, iota_lo, w2, gates, tok_idx, dst_idx, tile_expert, w2s):
    with ExitStack() as c:
        def sb(name, shape, dt):
            return c.enter_context(nc.sbuf_tensor(name, shape, dt))

        def sem(name):
            return c.enter_context(nc.semaphore(name))

        cf = sb("d_consts", [128, D_CONSTS], F32)
        tri_sb = sb("d_tri", [QT, 2, QT], BF16)
        i_hi = sb("d_iota_hi", [QT, HALVES], F32)
        i_lo = sb("d_iota_lo", [QT, 128], F32)
        top = sb("d_top", [QT, 2, TILES], F32)
        eq = sb("d_eq", [QT, TILES, E], F32)
        idx = sb("d_idx", [QT, TILES], F32)
        rest = sb("d_rest", [QT, TILES, E], F32)
        hot = sb("d_hot", [QT, BLOCKS, E], F32)
        hot_b = sb("d_hot_b", [QT, BLOCKS, E], BF16)
        diff = sb("d_diff", [QT, TILES], F32)
        ex = sb("d_ex", [QT, TILES], F32)
        total = sb("d_total", [QT, BLOCKS, E], F32)
        upto = sb("d_upto", [QT, BLOCKS, E], F32)
        ones = sb("d_ones", [QT, BLOCKS], F32)
        fill = sb("d_fill", [QT, E, MAXT], F32)
        n_t = sb("d_n_t", [QT, E], F32)
        n_cum = sb("d_n_cum", [QT, E], F32)
        base = sb("d_base", [QT, E], F32)
        past = sb("d_past", [QT, NT, E - 1], F32)
        te = sb("d_te", [QT, NT], F32)
        slot = sb("d_slot", [QT, BLOCKS], F32)
        slot_i = sb("d_slot_i", [QT, BLOCKS], I32)
        part_i = sb("d_part_i", [QT, 2, BLOCKS], I32)
        part = sb("d_part", [QT, 2, BLOCKS], F32)
        a_hot = sb("d_a_hot", [QT, 4, HALVES], F32)
        b_hot = sb("d_b_hot", [QT, 4, 128], F32)
        w_in = sb("d_w_in", [128, 2, WCH], F32)
        f = sb("d_f", [128, HALVES], F32)
        g = sb("d_g", [128, 2, HALVES], F32)
        ps = c.enter_context(nc.psum_tensor("d_ps", [128, 4, 512], F32))
        ps_i = c.enter_context(nc.psum_tensor("d_ps_i", [128, 512], F32))

        iota_m8 = cf[0:QT, 0:E]
        full_at = cf[0:QT, E:E + MAXT]
        tile_no = cf[0:QT, E + MAXT:E + MAXT + NT]
        value = cf[0:QT, E + MAXT + NT:E + MAXT + NT + BLOCKS]
        spare = cf[:, E + MAXT + NT + BLOCKS:E + MAXT + NT + BLOCKS + HALVES]

        c_in = sem("d_c_in")
        tri_in = sem("d_tri_in")
        did = sem("d_did")
        diff_ok = sem("d_diff_ok")
        ex_ok = sem("d_ex_ok")
        hot_ok = sem("d_hot_ok")
        cnt_ok = sem("d_cnt_ok")
        pair_ok = sem("d_pair_ok")
        pair_used = sem("d_pair_used")

        w_ld = [sem(f"d_w_ld{i}") for i in range(2)]
        w_hi = sem("d_w_hi")
        w_free = sem("d_w_free")

        def w2_part(n, e, s):
            return w2s[:, bass.ds(e, 1), n, s * WCH:(s + 1) * WCH].rearrange("p a n -> p (a n)")

        def per_e(t2):
            return t2.rearrange("p (a e) -> p a e", a=1)

        def over_e(t2, n):
            return t2.rearrange("p (t a) -> p t a", a=1).to_broadcast([QT, n, E])

        with nc.Block() as block:

            @block.sync
            def _(sp):
                sp.dma_start(cf[:, :], consts_f).then_inc(c_in, 16)
                sp.dma_start(i_hi[:, :], iota_hi).then_inc(c_in, 16)
                sp.dma_start(i_lo[:, :], iota_lo).then_inc(c_in, 16)
                sp.dma_start(tri_sb[:, :, :], tri).then_inc(tri_in, 16)

                def load_w2(s, e):
                    sp.dma_start(w_in[:, s], w2[:, bass.ds(e, 1), s * WCH:(s + 1) * WCH
                                                ].rearrange("p a n -> p (a n)")).then_inc(w_ld[s], 16)

                for s in range(2):
                    load_w2(s, 0)
                with sp.Fori(0, E - 1) as e:
                    for s in range(2):
                        sp.wait_ge(w_free, s + 1)
                        load_w2(s, e + 1)
                    sp.sem_inc(w_free, -2)

            @block.vector
            def _(dve):
                count = [0]

                def link(ins):
                    ins.then_inc(did, 1)
                    count[0] += 1
                    dve.wait_ge(did, count[0])

                dve.wait_ge(c_in, 48)
                link(dve.memset(ones[:, :], 1.0))
                lg = logits[:, :, :]
                for k in range(2):
                    one_hot = hot[:, k * TILES:(k + 1) * TILES, :]
                    link(dve.tensor_reduce(top[:, k, :], lg, AX.X, ALU.max))
                    link(dve.tensor_tensor(eq[:, :, :], lg, over_e(top[:, k, :], TILES), ALU.is_equal))
                    link(dve.tensor_tensor(eq[:, :, :], eq[:, :, :], per_e(iota_m8).to_broadcast([QT, TILES, E]),
                                           ALU.mult))
                    link(dve.tensor_reduce(idx[:, :], eq[:, :, :], AX.X, ALU.min))
                    link(dve.tensor_tensor(one_hot, per_e(iota_m8).to_broadcast([QT, TILES, E]),
                                           over_e(idx[:, :], TILES), ALU.is_equal))
                    if k == 0:
                        link(dve.scalar_tensor_tensor(rest[:, :, :], one_hot, -1e30, lg, ALU.mult, ALU.add))
                        lg = rest[:, :, :]
                dve.tensor_copy(hot_b[:, :, :], hot[:, :, :]).then_inc(hot_ok, 1)
                dve.tensor_tensor(diff[:, :], top[:, 1, :], top[:, 0, :], ALU.subtract).then_inc(diff_ok, 1)
                dve.wait_ge(cnt_ok, 1)
                for k in range(2):
                    link(dve.tensor_copy(total[:, k * TILES:(k + 1) * TILES, :],
                                         ps[0:QT, 2 + k, 0:TILES * E].rearrange("p (t e) -> p t e", e=E)))
                for e in range(E):
                    link(dve.tensor_tensor_scan(upto[:, :, e], ones[:, :], total[:, :, e], 0.0, ALU.mult, ALU.add))
                link(dve.tensor_tensor(fill[:, :, :], upto[:, BLOCKS - 1, :].rearrange("p (e a) -> p e a", a=1
                                                                                   ).to_broadcast([QT, E, MAXT]),
                                       full_at.rearrange("p (a n) -> p a n", a=1).to_broadcast([QT, E, MAXT]),
                                       ALU.is_gt))
                link(dve.tensor_reduce(n_t[:, :], fill[:, :, :], AX.X, ALU.add))
                link(dve.tensor_tensor_scan(n_cum[:, :], ones[:, 0:E], n_t[:, :], 0.0, ALU.mult, ALU.add))
                link(dve.tensor_tensor(base[:, :], n_cum[:, :], n_t[:, :], ALU.subtract))
                link(dve.tensor_scalar(base[:, :], base[:, :], float(ST), None, ALU.mult))
                link(dve.tensor_tensor(past[:, :, :], tile_no.rearrange("p (t a) -> p t a", a=1
                                                                      ).to_broadcast([QT, NT, E - 1]),
                                       per_e(n_cum[:, 0:E - 1]).to_broadcast([QT, NT, E - 1]), ALU.is_ge))
                link(dve.tensor_reduce(te[:, :], past[:, :, :], AX.X, ALU.add))
                link(dve.tensor_copy(tile_expert[0:1, :], te[0:1, :]))
                link(dve.tensor_tensor(upto[:, :, :], upto[:, :, :], total[:, :, :], ALU.subtract))
                for k in range(2):
                    half = upto[:, k * TILES:(k + 1) * TILES, :]
                    link(dve.tensor_tensor(half, ps[0:QT, k, 0:TILES * E].rearrange("p (t e) -> p t e", e=E), half,
                                           ALU.add))
                link(dve.tensor_tensor(upto[:, :, :], upto[:, :, :], per_e(base[:, :]).to_broadcast([QT, BLOCKS, E]),
                                       ALU.add))
                link(dve.tensor_tensor(upto[:, :, :], upto[:, :, :], hot[:, :, :], ALU.mult))
                link(dve.tensor_reduce(slot[:, :], upto[:, :, :], AX.X, ALU.add))
                link(dve.tensor_copy(slot_i[:, :], slot[:, :]))
                link(dve.tensor_scalar(part_i[:, 0, :], slot_i[:, :], 7, None, ALU.arith_shift_right))
                link(dve.tensor_scalar(part_i[:, 1, :], slot_i[:, :], 127, None, ALU.bitwise_and))
                link(dve.tensor_copy(part[:, :, :], part_i[:, :, :]))

                dve.wait_ge(ex_ok, 1)
                link(dve.tensor_scalar(top[:, 0, :], ex[:, :], 1.0, None, ALU.add))
                link(dve.reciprocal(gates[:, 0, :], top[:, 0, :]))
                link(dve.tensor_tensor(gates[:, 1, :], gates[:, 0, :], ex[:, :], ALU.mult))

                def one_hots(j, b):
                    dve.wait_ge(pair_used, j + 1)
                    dve.tensor_scalar(a_hot[:, j, :], i_hi[:, :], part[:, 0, bass.ds(b, 1)], value[:, bass.ds(b, 1)],
                                      ALU.is_equal, ALU.mult)
                    dve.tensor_scalar(b_hot[:, j, :], i_lo[:, :], part[:, 1, bass.ds(b, 1)], None, ALU.is_equal
                                      ).then_inc(pair_ok, 1)

                dve.sem_inc(pair_used, 4)
                with dve.Fori(0, BLOCKS // 4) as i:
                    for j in range(4):
                        one_hots(j, 4 * i + j)
                    dve.sem_inc(pair_used, -4)
                dve.wait_ge(pair_used, 4)
                link(dve.tensor_copy(f[:, :], ps_i[:, 0:HALVES]))
                link(dve.tensor_scalar(g[:, 0, :], f[:, :], 0.0, None, ALU.is_equal))
                link(dve.tensor_tensor(g[:, 0, :], g[:, 0, :], spare, ALU.mult))
                link(dve.tensor_tensor(g[:, 0, :], g[:, 0, :], f[:, :], ALU.add))
                link(dve.tensor_scalar(dst_idx[:, :], g[:, 0, :], -1.0, None, ALU.add))
                link(dve.tensor_scalar(g[:, 1, :], f[:, :], float(TOKENS), -float(TOKENS), ALU.is_gt, ALU.mult))
                link(dve.tensor_tensor(g[:, 1, :], g[:, 1, :], f[:, :], ALU.add))
                link(dve.tensor_scalar(tok_idx[:, :], g[:, 1, :], -1.0, 0.0, ALU.add, ALU.max))

            @block.scalar
            def _(act):
                act.wait_ge(diff_ok, 1)
                act.activation(ex[:, :], diff[:, :], ACT.Exp).then_inc(ex_ok, 1)
                with act.Fori(0, E) as e:
                    for s in range(2):
                        act.wait_ge(w_ld[s], 16)
                        act.sem_inc(w_ld[s], -16)
                        split_on_act(act, w_in[:, s], w2_part(0, e, s)).then_inc(w_hi, 1)

            @block.gpsimd
            def _(pool):
                with pool.Fori(0, E) as e:
                    for s in range(2):
                        pool.wait_ge(w_hi, 1)
                        pool.sem_inc(w_hi, -1)
                        pool.tensor_tensor(w2_part(1, e, s), w_in[:, s], w2_part(0, e, s), ALU.subtract
                                           ).then_inc(w_free, 1)

            @block.tensor
            def _(pe):
                pe.wait_ge(tri_in, 16)
                pe.wait_ge(hot_ok, 1)
                for n in range(2):
                    for k in range(2):
                        last = pe.matmul(ps[0:QT, 2 * n + k, 0:TILES * E], tri_sb[:, n, :],
                                         hot_b[:, k * TILES:(k + 1) * TILES, :].rearrange("p t e -> p (t e)"),
                                         start=True, stop=True)
                last.then_inc(cnt_ok, 1)

                def block_product(j, first, final):
                    pe.wait_ge(pair_ok, j + 1)
                    pe.matmul(ps_i[:, 0:HALVES], b_hot[:, j, :], a_hot[:, j, :], start=first, stop=final
                              ).then_inc(pair_used, 1)

                for j in range(4):
                    block_product(j, j == 0, False)
                pe.sem_inc(pair_ok, -4)
                with pe.Fori(1, BLOCKS // 4 - 1):
                    for j in range(4):
                        block_product(j, False, False)
                    pe.sem_inc(pair_ok, -4)
                for j in range(4):
                    block_product(j, False, j == 3)


def routing_constants():
    import numpy as np
    p = np.arange(128)[:, None]
    parts = [np.arange(E)[None] - E + 0 * p, ST * np.arange(MAXT)[None] + 0 * p, np.arange(NT)[None] + 0 * p,
             np.arange(BLOCKS)[None] * QT + p + 1, CHOICES + 1 + 128 * np.arange(HALVES)[None] + p]
    tri = np.zeros((QT, 2, QT), np.float32)
    tri[:, 0, :] = np.arange(QT)[:, None] < np.arange(QT)[None]
    tri[:, 1, :] = 1
    return np.concatenate(parts, 1).astype(np.float32), tri


D_CONSTS = E + MAXT + NT + BLOCKS + HALVES


def stage_e(nc, xs_dram, y_dram, w1s, w2s, b1, b2, ident16, tok_idx, dst_idx, tile_expert):
    with ExitStack() as c:
        def sb(name, shape, dt):
            return c.enter_context(nc.sbuf_tensor(name, shape, dt))

        def sem(name):
            return c.enter_context(nc.semaphore(name))

        U = 4
        id_e = sb("e_ident", [128, 128], F16)
        b1_sb = sb("e_b1", [128, E * HC], F32)
        b2_sb = sb("e_b2", [128, E, C], F32)
        xg = sb("e_xg", [128, U, 2, 2 * C], F16)
        xt = sb("e_xt", [128, 2, 2, 4, 128], F16)
        gf = sb("e_gf", [128, 4, ST], F32)
        g_hi = sb("e_g_hi", [128, 2, HC, ST], F16)
        g_lo = sb("e_g_lo", [128, 2, HC, ST], F16)
        y_sb = sb("e_y", [128, 2, 2, C], F32)
        gi = sb("e_gi", [128, U, 2], I32)
        si = sb("e_si", [128, 2, 2], I32)
        ps_x = c.enter_context(nc.psum_tensor("e_ps_x", [128, 2 * 4 * 128], F16))
        ps_h = c.enter_context(nc.psum_tensor("e_ps_h", [128, 4, 512], F32))
        ps_y = c.enter_context(nc.psum_tensor("e_ps_y", [128, 2, 512], F32))

        id_in = sem("e_id_in")
        b1_in = sem("e_b1_in")
        b2_in = sem("e_b2_in")
        idx_ok = sem("e_idx_ok")
        xg_in = [sem(f"e_xg_in{i}") for i in range(U)]
        x_tr = sem("e_x_tr")
        xt_ok = sem("e_xt_ok")
        h_ok = sem("e_h_ok")
        g_ok = sem("e_g_ok")
        hi_ok = sem("e_hi_ok")
        gs_ok = sem("e_gs_ok")
        y_ok = sem("e_y_ok")
        y_out = sem("e_y_out")
        y_done = [sem(f"e_y_done{i}") for i in range(2)]

        with nc.Block() as block:

            @block.sync
            def _(sp):
                sp.dma_start(id_e[:, :], ident16).then_inc(id_in, 16)
                sp.dma_start(b1_sb[:, :], b1).then_inc(b1_in, 16)
                sp.dma_start(b2_sb[:, :, :].rearrange("p e c -> p (e c)"), b2.to_broadcast([128, E * C])
                             ).then_inc(b2_in, 16)

            @block.gpsimd
            def _(pool):
                def fetch_indices(dst, src, n):
                    pool.tensor_copy(dst, src[:, bass.ds(2 * n, 2)]).then_inc(idx_ok, 1)
                    pool.wait_ge(idx_ok, 1)
                    pool.sem_inc(idx_ok, -1)

                def gather(j, n):
                    fetch_indices(gi[:, j, :], tok_idx, n)
                    for h in range(2):
                        pool.indirect_dma_start(out=xg[:, j, h, :], out_offset=None, in_=xs_dram,
                                                in_offset=bass.IndirectOffsetOnAxis(ap=gi[:, j, h:h + 1], axis=0)
                                                ).then_inc(xg_in[j], 16)

                def step(j, n, last):
                    s = j % 2
                    pool.wait_ge(y_out, j + 1)
                    fetch_indices(si[:, s, :], dst_idx, n)
                    for h in range(2):
                        pool.indirect_dma_start(out=y_dram,
                                                out_offset=bass.IndirectOffsetOnAxis(ap=si[:, s, h:h + 1], axis=0),
                                                in_=y_sb[:, s, h, :], in_offset=None).then_inc(y_done[s], 16)
                    if not last:
                        gather(j, n + U)

                for j in range(U):
                    gather(j, j)
                with pool.Fori(0, NT // U - 1) as i:
                    for j in range(U):
                        step(j, U * i + j, False)
                    pool.sem_inc(y_out, -U)
                for j in range(U):
                    step(j, NT - U + j, True)

            @block.tensor
            def _(pe):
                pe.wait_ge(id_in, 16)

                def turn(m, round_):
                    pe.wait_ge(xg_in[m % U], 32 * round_)
                    for h in range(2):
                        for q in range(4):
                            last = pe.transpose(ps_x[:, (4 * h + q) * 128:(4 * h + q + 1) * 128],
                                                xg[:, m % U, h, q * 128:(q + 1) * 128], id_e[:, :])
                    last.then_inc(x_tr, 1)

                def up(m, e, first):
                    s = m % 2
                    pe.wait_ge(xt_ok, 1)
                    pe.sem_inc(xt_ok, -1)
                    for hc in range(HC):
                        if not first or hc >= 4:
                            pe.wait_ge(gs_ok, hc - 3 + (0 if first else HC))
                        n = 0
                        for k in range(KC):
                            for w, p in ((0, 0), (0, 1), (1, 0)):
                                a = k * FH + hc * 128
                                mm = pe.matmul(ps_h[:, hc % 4, 0:ST],
                                               w1s[:, bass.ds(e, 1), w, a:a + 128].rearrange("p a n -> p (a n)"),
                                               xt[:, s, :, 2 * p + k, :], start=n == 0, stop=n == 3 * KC - 1)
                                n += 1
                        mm.then_inc(h_ok, 1)
                    if not first:
                        pe.sem_inc(gs_ok, -HC)

                def down(m, e):
                    s = m % 2
                    for h in range(2):
                        n = 0
                        for hc in range(HC):
                            for g, w in ((g_hi, 0), (g_hi, 1), (g_lo, 0)):
                                a = hc * C
                                mm = pe.matmul(ps_y[:, s, h * C:(h + 1) * C], g[:, s, hc, h * 128:(h + 1) * 128],
                                               w2s[:, bass.ds(e, 1), w, a:a + C].rearrange("p a n -> p (a n)"),
                                               start=n == 0, stop=n == 3 * HC - 1)
                                n += 1
                    mm.then_inc(y_ok, 1)

                def expert(n):
                    return pe.value_load(tile_expert[0:1, bass.ds(n, 1)], min_val=0, max_val=E - 1)

                turn(0, 1)
                up(0, expert(0), True)
                turn(1, 1)
                with pe.Fori(0, NT // U - 1) as i:
                    for j in range(U):
                        up(j + 1, expert(U * i + j + 1), False)
                        turn(j + 2, i + 1 + (j + 2) // U)
                        down(j, expert(U * i + j))
                for j in range(U):
                    n = NT - U + j
                    if j + 1 < U:
                        up(j + 1, expert(n + 1), False)
                    else:
                        pe.wait_ge(gs_ok, HC)
                    if j + 2 < U:
                        turn(j + 2, NT // U)
                    down(j, expert(n))

            @block.scalar
            def _(act):
                act.wait_ge(b1_in, 16)
                with act.Fori(0, NT // 2) as i:
                    for j in range(2):
                        e = act.value_load(tile_expert[0:1, bass.ds(2 * i + j, 1)], min_val=0, max_val=E - 1)
                        for hc in range(HC):
                            act.wait_ge(h_ok, j * HC + hc + 1)
                            act.activation(gf[:, hc % 4, :], ps_h[:, hc % 4, 0:ST], ACT.Gelu,
                                           bias=b1_sb[:, bass.ds(e * HC + hc, 1)], scale=1.0 / WSCALE).then_inc(g_ok, 1)
                    act.sem_inc(h_ok, -2 * HC)

            @block.vector
            def _(dve):
                dve.wait_ge(b2_in, 16)

                def take_x(s):
                    dve.wait_ge(x_tr, 1)
                    dve.sem_inc(x_tr, -1)
                    dve.tensor_copy(xt[:, s].rearrange("p h q n -> p (h q n)").bitcast(I32), ps_x[:, :].bitcast(I32)
                                    ).then_inc(xt_ok, 1)

                def split(s):
                    for hc in range(HC):
                        dve.wait_ge(g_ok, hc + 1)
                        dve.tensor_copy(g_hi[:, s, hc, :], gf[:, hc % 4, :]).then_inc(hi_ok, 1)
                        dve.wait_ge(hi_ok, hc + 1)
                        dve.tensor_tensor(g_lo[:, s, hc, :], gf[:, hc % 4, :], g_hi[:, s, hc, :], ALU.subtract
                                          ).then_inc(gs_ok, 1)
                    dve.sem_inc(g_ok, -HC)
                    dve.sem_inc(hi_ok, -HC)

                def take_y(s, n, scatters):
                    e = dve.value_load(tile_expert[0:1, bass.ds(n, 1)], min_val=0, max_val=E - 1)
                    if scatters is not None:
                        dve.wait_ge(y_done[s], 32 * scatters)
                    dve.wait_ge(y_ok, 1)
                    dve.sem_inc(y_ok, -1)
                    dve.scalar_tensor_tensor(y_sb[:, s], ps_y[:, s, :].rearrange("p (h c) -> p h c", h=2),
                                             1.0 / WSCALE, b2_sb[:, bass.ds(e, 1), :].to_broadcast([128, 2, C]),
                                             ALU.mult, ALU.add).then_inc(y_out, 1)

                take_x(0)
                split(0)
                take_x(1)
                for j in range(2):
                    split(1 - j)
                    take_x(j)
                    take_y(j, j, None)
                with dve.Fori(1, NT // 2 - 1) as i:
                    for j in range(2):
                        split(1 - j)
                        take_x(j)
                        take_y(j, 2 * i + j, i)
                split(1)
                take_y(0, NT - 2, NT // 2 - 1)
                take_y(1, NT - 1, NT // 2 - 1)
                for s in range(2):
                    dve.wait_ge(y_done[s], 32 * (NT // 2))


def stage_f(nc, x1_dram, y_dram, gates, out):
    with ExitStack() as c:
        def sb(name, shape, dt):
            return c.enter_context(nc.sbuf_tensor(name, shape, dt))

        def sem(name):
            return c.enter_context(nc.semaphore(name))

        U = 2
        x1 = sb("f_x1", [QT, U, TPG, C], F32)
        y = sb("f_y", [QT, U, 2, TPG, C], F32)
        t1 = sb("f_t", [QT, U, TPG, C], F32)
        o = sb("f_o", [QT, U, TPG, C], F32)
        in_ok = [sem(f"f_in{i}") for i in range(U)]
        half_ok = sem("f_half")

        stored = [sem(f"f_stored{i}") for i in range(U)]
        used = sem("f_used")

        def rows(t, tok):
            return t[bass.ds(tok, BAND), :].rearrange("(t p) c -> p t c", p=QT)

        with nc.Block() as block:

            @block.sync
            def _(sp):
                def load(s, tok):
                    sp.dma_start(x1[:, s], rows(x1_dram, tok)).then_inc(in_ok[s], 16)
                    for k in range(2):
                        sp.dma_start(y[:, s, k], rows(y_dram, tok + k * TOKENS)).then_inc(in_ok[s], 16)

                for s in range(U):
                    load(s, s * BAND)
                with sp.Fori(0, GROUPS // U - 1) as i:
                    for s in range(U):
                        sp.wait_ge(used, s + 1)
                        sp.dma_start(rows(out, (U * i + s) * BAND), o[:, s]).then_inc(stored[s], 16)
                        load(s, (U * i + s + U) * BAND)
                    sp.sem_inc(used, -U)
                for s in range(U):
                    sp.wait_ge(used, s + 1)
                    sp.dma_start(rows(out, (GROUPS - U + s) * BAND), o[:, s]).then_inc(stored[s], 16)

            @block.vector
            def _(dve):
                for s in range(U):
                    dve.sem_inc(stored[s], 16)
                with dve.Fori(0, GROUPS // U) as i:
                    for s in range(U):
                        dve.wait_ge(in_ok[s], 48)
                        dve.sem_inc(in_ok[s], -48)
                        dve.wait_ge(stored[s], 16)
                        dve.sem_inc(stored[s], -16)
                        for k, (dst, src, done) in enumerate(((t1, x1, half_ok), (o, t1, used))):
                            for t in range(TPG):
                                last = dve.scalar_tensor_tensor(dst[:, s, t, :], y[:, s, k, t, :],
                                                                gates[:, k, bass.ds((U * i + s) * TPG + t, 1)],
                                                                src[:, s, t, :], ALU.mult, ALU.add)
                            last.then_inc(done, 1)
                            if k == 0:
                                dve.wait_ge(half_ok, 1)
                                dve.sem_inc(half_ok, -1)
                for s in range(U):
                    dve.wait_ge(stored[s], 16)


def col_windows(q):
    s = min(max(q - HALF, 0), W - WIN)
    return s, s + WIN


def masks():
    import numpy as np
    q = np.zeros((32, QR, W), np.float16)
    for i in range(QR):
        q[i, i, :] = 1
    for w in range(W):
        q[QR + w % MODC, :, w] = 1
    k = np.full((3, 32, KR, W), NEG, np.float16)
    for cls, r in enumerate((0, 1, BANDS - 1)):
        r0 = QR * r + row_offset(r)
        for i in range(QR):
            s = min(max(QR * r + i - HALF, 0), H - WIN) - r0
            k[cls, i, s:s + WIN, :] = 0
    for w in range(W):
        a, b = col_windows(w)
        k[:, QR + w % MODC, :, a:b] = 0
    return q.reshape(32, QR, COLS, QC).transpose(0, 2, 1, 3).reshape(32, BAND), k.reshape(3, 32, KR * W)


def program(nc, t, out):
    def scratch(name, shape, dt):
        return nc.dram_tensor(name, shape, dt, kind="Internal").ap()

    qk_hi = scratch("qk_hi", [128, 4, TOKENS], F16)
    qk_lo = scratch("qk_lo", [128, 4, TOKENS], F16)
    v_rows = scratch("v_rows", [TOKENS, 2 * C], F16)
    rpb_pad = scratch("rpb_pad", [NH, PAD_R, PAD_C], F32)
    rpb_cols = scratch("rpb_cols", [QC, NH, PAD_R, BIAS_C], F32)
    attn = scratch("attn", [TOKENS, C], F32)
    x1 = scratch("x1", [TOKENS, C], F32)
    xs = scratch("xs", [TOKENS, 2 * C], F16)
    y = scratch("y", [CHOICES + SLOTS, C], F32)

    with ExitStack() as c:
        w1s = c.enter_context(nc.sbuf_tensor("w1s", [128, E, 2, EW], F16))
        with nc.sbuf_tensor("bias", [QT, NH, BIAS_R, BIAS_C], F32) as bias:
            stage_a(nc, t["x"], t["wqkv"], t["bqk"], t["bv"], t["rpb"], t["w1"], t["ident"], rpb_pad, rpb_cols,
                    qk_hi, qk_lo, v_rows, bias, w1s)
            stage_b(nc, qk_hi, qk_lo, v_rows, bias, t["q_mask"], t["k_mask"], t["ident16"], attn)
        w2s = c.enter_context(nc.sbuf_tensor("w2s", [128, E, 2, EW], F16))
        logits = c.enter_context(nc.sbuf_tensor("logits", [QT, TILES, E], F32))
        gates = c.enter_context(nc.sbuf_tensor("gates", [QT, 2, TILES], F32))
        tok_idx = c.enter_context(nc.sbuf_tensor("tok_idx", [128, HALVES], I32))
        dst_idx = c.enter_context(nc.sbuf_tensor("dst_idx", [128, HALVES], I32))
        tile_expert = c.enter_context(nc.sbuf_tensor("tile_expert", [1, NT], I32))
        stage_c(nc, t["x"], attn, t["wproj"], t["bproj"], t["wg"], t["bg"], t["ident"], x1, xs, logits)
        stage_d(nc, logits, t["consts"], t["tri"], t["iota_hi"], t["iota_lo"], t["w2"], gates, tok_idx, dst_idx,
                tile_expert, w2s)
        stage_e(nc, xs, y, w1s, w2s, t["b1"], t["b2"], t["ident16"], tok_idx, dst_idx, tile_expert)
        stage_f(nc, x1, y, gates, out)


def kernel(**inputs):
    import ml_dtypes
    import numpy as np
    import concourse.bacc as bacc
    from concourse.bass_utils import run_bass_kernel_spmd as run

    q_mask, k_mask = masks()
    consts, tri = routing_constants()
    arrays = {
        "x": np.transpose(inputs["x"], (0, 2, 3, 1)).reshape(TOKENS, C),
        "wqkv": inputs["L0_conv_w_qkv"].T.reshape(KC, 128, 3 * C).transpose(1, 0, 2),
        "bqk": inputs["L0_conv_b_qkv"][:2 * C].reshape(4, 128).T,
        "bv": inputs["L0_conv_b_qkv"][2 * C:].reshape(1, C),
        "rpb": inputs["L0_conv_rpb"],
        "wproj": inputs["L0_conv_w_proj"].T.reshape(KC, 128, C).transpose(1, 0, 2),
        "bproj": inputs["L0_conv_b_proj"].reshape(1, C),
        "wg": inputs["L0_ffn_Wg"].reshape(KC, 128, E).transpose(1, 0, 2),
        "bg": inputs["L0_ffn_bg"].reshape(1, E),
        "w1": inputs["L0_ffn_W1"].reshape(E, KC, 128, FH).transpose(2, 0, 1, 3).reshape(128, E, EW),
        "b1": inputs["L0_ffn_b1"].reshape(E * HC, 128).T,
        "w2": inputs["L0_ffn_W2"].reshape(E, HC, 128, C).transpose(2, 0, 1, 3).reshape(128, E, EW),
        "b2": inputs["L0_ffn_b2"].reshape(1, E * C),
        "ident": np.eye(128, dtype=np.float32),
        "ident16": np.eye(128, dtype=np.float16),
        "q_mask": q_mask,
        "k_mask": k_mask,
        "consts": consts,
        "tri": tri.astype(ml_dtypes.bfloat16),
        "iota_hi": np.tile(np.arange(HALVES, dtype=np.float32), (QT, 1)),
        "iota_lo": np.tile(np.arange(128, dtype=np.float32), (QT, 1)),
    }
    arrays = {f"in_{n}": np.ascontiguousarray(a) for n, a in arrays.items()}
    nc = bacc.Bacc("TRN2", target_bir_lowering=False, num_devices=1, dynamic_dma_scratch_size=4096)
    t = {n[3:]: nc.dram_tensor(n, a.shape, mybir.dt.from_np(a.dtype), kind="ExternalInput").ap()
         for n, a in arrays.items()}
    out = nc.dram_tensor("out", [TOKENS, C], F32, kind="ExternalOutput").ap()
    program(nc, t, out)
    got = run(nc, [arrays], core_ids=[0]).results[0]["out"]
    return np.ascontiguousarray(np.transpose(got.reshape(B, H, W, C), (0, 3, 1, 2)))
```
